# Optimizing a Trainium2 kernel written in Bass

```python
import numpy as np
import jax
import jax.numpy as jnp

def _softmax(x, axis=-1):
    return jax.nn.softmax(x, axis=axis)

def _gelu(x):
    return jax.nn.gelu(x, approximate=True)

def _silu(x):
    return jax.nn.silu(x)

def _sigmoid(x):
    return jax.nn.sigmoid(x)

def _layernorm(x, axis=-1, eps=1e-05):
    m = jnp.mean(x, axis=axis, keepdims=True)
    v = jnp.var(x, axis=axis, keepdims=True)
    return (x - m) / jnp.sqrt(v + eps)

def _scatter_add(tgt, idx, src, axis=0):
    return tgt.at[idx].add(src)

def _segment_sum(src, seg, n):
    return jax.ops.segment_sum(src, seg, n)
kernel_name = 'mk_xattn_seq_d2_seqx_r2_32ed6f'

def setup_inputs(seed: int=0):
    np.random.seed(seed)
    _w = jnp.asarray

    def _rec_inputs():
        import jax
        import jax.numpy as jnp
        _rk = jax.random.key(seed)
        x = -0.0002928 + 1 * jax.random.normal(jax.random.fold_in(_rk, 1), (16, 256, 512), jnp.float32)
        _lenS = 256 - jax.random.randint(jax.random.fold_in(_rk, 7), (16,), 0, max(1, 256 // 4) + 1, jnp.int32)
        _lenS2 = 256 - jax.random.randint(jax.random.fold_in(_rk, 8), (16,), 0, max(1, 256 // 4) + 1, jnp.int32)
        _ctx_1024P = jax.random.normal(jax.random.fold_in(_rk, 11), (16, 16, 512), jnp.float32)
        _ctx_1024c = jax.random.dirichlet(jax.random.fold_in(_rk, 511), 0.3 * jnp.ones((16,), jnp.float32), (16, 256))
        _ctx_1024t = jnp.einsum('bsk,bkd->bsd', _ctx_1024c, _ctx_1024P)
        _ctx_1024t = _ctx_1024t * jax.lax.rsqrt(jnp.mean(jnp.square(_ctx_1024t)) + 1e-12) * 0.953939
        ctx_1024 = -1.39393e-06 + 0.999914 * (_ctx_1024t + 0.3 * jax.random.normal(jax.random.fold_in(_rk, 611), (16, 256, 512), jnp.float32))
        _validS = jnp.arange(256)[None, :] < _lenS[:, None]
        _validS2 = jnp.arange(256)[None, :] < _lenS2[:, None]
        _causal = jnp.tril(jnp.ones((256, 256), dtype=bool))
        mask_Bx1x1xS2_if1 = jnp.where(jnp.ones((16, 1, 1, 256), dtype=bool), 1, 0).astype(jnp.int32)
        mask_Bx1xSxS2_if1 = jnp.where(jnp.ones((16, 1, 256, 256), dtype=bool), 1, 0).astype(jnp.int32)
        return (x, ctx_1024, mask_Bx1x1xS2_if1, mask_Bx1xSxS2_if1)
    x, ctx_1024, mask_Bx1x1xS2_if1, mask_Bx1xSxS2_if1 = _rec_inputs()

    def _L0_xattn_setup():
        import jax, jax.numpy as jnp
        import numpy as np
        B, Q, KV = (2, 1024, 1024)
        D_MODEL = 512
        N_HEADS = 16
        D_KV = 64
        EPS = 1e-06
        key = jax.random.key(seed)
        ks = jax.random.split(key, 7)
        s = 0.02
        return {'hidden_states': jax.random.normal(ks[0], (B, Q, D_MODEL), jnp.float32), 'key_value_states': jax.random.normal(ks[1], (B, KV, D_MODEL), jnp.float32), 'wq': jax.random.normal(ks[2], (D_MODEL, N_HEADS * D_KV), jnp.float32) * s, 'wk': jax.random.normal(ks[3], (D_MODEL, N_HEADS * D_KV), jnp.float32) * s, 'wv': jax.random.normal(ks[4], (D_MODEL, N_HEADS * D_KV), jnp.float32) * s, 'wo': jax.random.normal(ks[5], (N_HEADS * D_KV, D_MODEL), jnp.float32) * s, 'norm_w': jnp.ones((D_MODEL,), jnp.float32)}
    _L0_xattn_all = _L0_xattn_setup()
    _L0_xattn_in = {k: v for k, v in _L0_xattn_all.items() if k in ('wq', 'wk', 'wv', 'wo', 'norm_w')}
    del _L0_xattn_all

    def _L1_xattn_setup():
        import jax, jax.numpy as jnp
        import numpy as np
        D_MODEL = 512
        NUM_HEADS = 16
        D_FF = 2048
        D_K = D_MODEL // NUM_HEADS
        LN_EPS = 1e-05

        def _linear(x, w, b):
            return jnp.einsum('bsd,od->bso', x, w) + b

        def _layernorm(x, g, b):
            mu = jnp.mean(x, axis=-1, keepdims=True)
            var = jnp.mean(jnp.square(x - mu), axis=-1, keepdims=True)
            return (x - mu) * jax.lax.rsqrt(var + LN_EPS) * g + b

        def _mha(q_in, kv_in, mask, wq, bq, wk, bk, wv, bv, wo, bo):
            B, Sq, _ = q_in.shape
            Sk = kv_in.shape[1]
            q = _linear(q_in, wq, bq).reshape(B, Sq, NUM_HEADS, D_K).transpose(0, 2, 1, 3)
            k = _linear(kv_in, wk, bk).reshape(B, Sk, NUM_HEADS, D_K).transpose(0, 2, 1, 3)
            v = _linear(kv_in, wv, bv).reshape(B, Sk, NUM_HEADS, D_K).transpose(0, 2, 1, 3)
            scores = jnp.einsum('bhqd,bhkd->bhqk', q, k) / jnp.sqrt(jnp.asarray(D_K, q.dtype))
            scores = jnp.where(mask == 0, jnp.asarray(-1000000000.0, scores.dtype), scores)
            attn = jax.nn.softmax(scores, axis=-1)
            out = jnp.einsum('bhqk,bhkd->bhqd', attn, v)
            out = out.transpose(0, 2, 1, 3).reshape(B, Sq, D_MODEL)
            return _linear(out, wo, bo)
        key = jax.random.key(seed)
        ks = jax.random.split(key, 24)
        B, S = (4, 1024)
        s = 0.02
        d = {'tgt': jax.random.normal(ks[0], (B, S, D_MODEL), jnp.float32), 'enc_output': jax.random.normal(ks[1], (B, S, D_MODEL), jnp.float32), 'src_mask': jnp.ones((B, 1, 1, S), jnp.int32), 'tgt_mask': jnp.ones((B, 1, S, S), jnp.int32)}
        names = ['sa_wq', 'sa_wk', 'sa_wv', 'sa_wo', 'ca_wq', 'ca_wk', 'ca_wv', 'ca_wo']
        for i, n in enumerate(names):
            d[n] = jax.random.normal(ks[2 + i], (D_MODEL, D_MODEL), jnp.float32) * s
            d[n.replace('w', 'b')] = jnp.zeros((D_MODEL,), jnp.float32)
        d['ffn_w1'] = jax.random.normal(ks[10], (D_FF, D_MODEL), jnp.float32) * s
        d['ffn_b1'] = jnp.zeros((D_FF,), jnp.float32)
        d['ffn_w2'] = jax.random.normal(ks[11], (D_MODEL, D_FF), jnp.float32) * s
        d['ffn_b2'] = jnp.zeros((D_MODEL,), jnp.float32)
        for i in (1, 2, 3):
            d[f'ln{i}_g'] = jnp.ones((D_MODEL,), jnp.float32)
            d[f'ln{i}_b'] = jnp.zeros((D_MODEL,), jnp.float32)
        return d
    _L1_xattn_all = _L1_xattn_setup()
    _L1_xattn_in = {k: v for k, v in _L1_xattn_all.items() if k in ('sa_wq', 'sa_bq', 'sa_wk', 'sa_bk', 'sa_wv', 'sa_bv', 'sa_wo', 'sa_bo', 'ca_wq', 'ca_bq', 'ca_wk', 'ca_bk', 'ca_wv', 'ca_bv', 'ca_wo', 'ca_bo', 'ffn_w1', 'ffn_b1', 'ffn_w2', 'ffn_b2', 'ln1_g', 'ln1_b', 'ln2_g', 'ln2_b', 'ln3_g', 'ln3_b')}
    del _L1_xattn_all
    return {'x': x, 'ctx_1024': ctx_1024, 'mask_Bx1x1xS2_if1': mask_Bx1x1xS2_if1, 'mask_Bx1xSxS2_if1': mask_Bx1xSxS2_if1, 'L0_xattn_wq': _L0_xattn_in['wq'], 'L0_xattn_wk': _L0_xattn_in['wk'], 'L0_xattn_wv': _L0_xattn_in['wv'], 'L0_xattn_wo': _L0_xattn_in['wo'], 'L0_xattn_norm_w': _L0_xattn_in['norm_w'], 'L1_xattn_sa_wq': _L1_xattn_in['sa_wq'], 'L1_xattn_sa_bq': _L1_xattn_in['sa_bq'], 'L1_xattn_sa_wk': _L1_xattn_in['sa_wk'], 'L1_xattn_sa_bk': _L1_xattn_in['sa_bk'], 'L1_xattn_sa_wv': _L1_xattn_in['sa_wv'], 'L1_xattn_sa_bv': _L1_xattn_in['sa_bv'], 'L1_xattn_sa_wo': _L1_xattn_in['sa_wo'], 'L1_xattn_sa_bo': _L1_xattn_in['sa_bo'], 'L1_xattn_ca_wq': _L1_xattn_in['ca_wq'], 'L1_xattn_ca_bq': _L1_xattn_in['ca_bq'], 'L1_xattn_ca_wk': _L1_xattn_in['ca_wk'], 'L1_xattn_ca_bk': _L1_xattn_in['ca_bk'], 'L1_xattn_ca_wv': _L1_xattn_in['ca_wv'], 'L1_xattn_ca_bv': _L1_xattn_in['ca_bv'], 'L1_xattn_ca_wo': _L1_xattn_in['ca_wo'], 'L1_xattn_ca_bo': _L1_xattn_in['ca_bo'], 'L1_xattn_ffn_w1': _L1_xattn_in['ffn_w1'], 'L1_xattn_ffn_b1': _L1_xattn_in['ffn_b1'], 'L1_xattn_ffn_w2': _L1_xattn_in['ffn_w2'], 'L1_xattn_ffn_b2': _L1_xattn_in['ffn_b2'], 'L1_xattn_ln1_g': _L1_xattn_in['ln1_g'], 'L1_xattn_ln1_b': _L1_xattn_in['ln1_b'], 'L1_xattn_ln2_g': _L1_xattn_in['ln2_g'], 'L1_xattn_ln2_b': _L1_xattn_in['ln2_b'], 'L1_xattn_ln3_g': _L1_xattn_in['ln3_g'], 'L1_xattn_ln3_b': _L1_xattn_in['ln3_b']}

def reference(x, ctx_1024, mask_Bx1x1xS2_if1, mask_Bx1xSxS2_if1, L0_xattn_wq, L0_xattn_wk, L0_xattn_wv, L0_xattn_wo, L0_xattn_norm_w, L1_xattn_sa_wq, L1_xattn_sa_bq, L1_xattn_sa_wk, L1_xattn_sa_bk, L1_xattn_sa_wv, L1_xattn_sa_bv, L1_xattn_sa_wo, L1_xattn_sa_bo, L1_xattn_ca_wq, L1_xattn_ca_bq, L1_xattn_ca_wk, L1_xattn_ca_bk, L1_xattn_ca_wv, L1_xattn_ca_bv, L1_xattn_ca_wo, L1_xattn_ca_bo, L1_xattn_ffn_w1, L1_xattn_ffn_b1, L1_xattn_ffn_w2, L1_xattn_ffn_b2, L1_xattn_ln1_g, L1_xattn_ln1_b, L1_xattn_ln2_g, L1_xattn_ln2_b, L1_xattn_ln3_g, L1_xattn_ln3_b):
    import jax
    import jax.numpy as jnp

    def _L0_xattn_ref(hidden_states, key_value_states, wq, wk, wv, wo, norm_w):
        import jax, jax.numpy as jnp
        import numpy as np
        B, Q, KV = (2, 1024, 1024)
        D_MODEL = 512
        N_HEADS = 16
        D_KV = 64
        EPS = 1e-06
        var = jnp.mean(jnp.square(hidden_states), axis=-1, keepdims=True)
        normed = hidden_states * jax.lax.rsqrt(var + EPS) * norm_w
        b, q_len, _ = hidden_states.shape
        kv_len = key_value_states.shape[1]

        def split_heads(x):
            return x.reshape(b, -1, N_HEADS, D_KV).transpose(0, 2, 1, 3)
        q = split_heads(normed @ wq)
        k = split_heads(key_value_states @ wk)
        v = split_heads(key_value_states @ wv)
        scores = jnp.einsum('bhqd,bhkd->bhqk', q, k)
        attn = jax.nn.softmax(scores.astype(jnp.float32), axis=-1).astype(scores.dtype)
        ctx = jnp.einsum('bhqk,bhkd->bhqd', attn, v)
        ctx = ctx.transpose(0, 2, 1, 3).reshape(b, q_len, N_HEADS * D_KV)
        attn_out = ctx @ wo
        return hidden_states + attn_out

    def _L1_xattn_ref(tgt, enc_output, src_mask, tgt_mask, sa_wq, sa_bq, sa_wk, sa_bk, sa_wv, sa_bv, sa_wo, sa_bo, ca_wq, ca_bq, ca_wk, ca_bk, ca_wv, ca_bv, ca_wo, ca_bo, ffn_w1, ffn_b1, ffn_w2, ffn_b2, ln1_g, ln1_b, ln2_g, ln2_b, ln3_g, ln3_b):
        import jax, jax.numpy as jnp
        import numpy as np
        D_MODEL = 512
        NUM_HEADS = 16
        D_FF = 2048
        D_K = D_MODEL // NUM_HEADS
        LN_EPS = 1e-05

        def _linear(x, w, b):
            return jnp.einsum('bsd,od->bso', x, w) + b

        def _layernorm(x, g, b):
            mu = jnp.mean(x, axis=-1, keepdims=True)
            var = jnp.mean(jnp.square(x - mu), axis=-1, keepdims=True)
            return (x - mu) * jax.lax.rsqrt(var + LN_EPS) * g + b

        def _mha(q_in, kv_in, mask, wq, bq, wk, bk, wv, bv, wo, bo):
            B, Sq, _ = q_in.shape
            Sk = kv_in.shape[1]
            q = _linear(q_in, wq, bq).reshape(B, Sq, NUM_HEADS, D_K).transpose(0, 2, 1, 3)
            k = _linear(kv_in, wk, bk).reshape(B, Sk, NUM_HEADS, D_K).transpose(0, 2, 1, 3)
            v = _linear(kv_in, wv, bv).reshape(B, Sk, NUM_HEADS, D_K).transpose(0, 2, 1, 3)
            scores = jnp.einsum('bhqd,bhkd->bhqk', q, k) / jnp.sqrt(jnp.asarray(D_K, q.dtype))
            scores = jnp.where(mask == 0, jnp.asarray(-1000000000.0, scores.dtype), scores)
            attn = jax.nn.softmax(scores, axis=-1)
            out = jnp.einsum('bhqk,bhkd->bhqd', attn, v)
            out = out.transpose(0, 2, 1, 3).reshape(B, Sq, D_MODEL)
            return _linear(out, wo, bo)
        t2 = _mha(tgt, tgt, tgt_mask, sa_wq, sa_bq, sa_wk, sa_bk, sa_wv, sa_bv, sa_wo, sa_bo)
        x = _layernorm(tgt + t2, ln1_g, ln1_b)
        t2 = _mha(x, enc_output, src_mask, ca_wq, ca_bq, ca_wk, ca_bk, ca_wv, ca_bv, ca_wo, ca_bo)
        x = _layernorm(x + t2, ln2_g, ln2_b)
        t2 = _linear(jax.nn.relu(_linear(x, ffn_w1, ffn_b1)), ffn_w2, ffn_b2)
        return _layernorm(x + t2, ln3_g, ln3_b)
    x = _L0_xattn_ref(x, ctx_1024, L0_xattn_wq, L0_xattn_wk, L0_xattn_wv, L0_xattn_wo, L0_xattn_norm_w)
    x = _L1_xattn_ref(x, ctx_1024, mask_Bx1x1xS2_if1, mask_Bx1xSxS2_if1, L1_xattn_sa_wq, L1_xattn_sa_bq, L1_xattn_sa_wk, L1_xattn_sa_bk, L1_xattn_sa_wv, L1_xattn_sa_bv, L1_xattn_sa_wo, L1_xattn_sa_bo, L1_xattn_ca_wq, L1_xattn_ca_bq, L1_xattn_ca_wk, L1_xattn_ca_bk, L1_xattn_ca_wv, L1_xattn_ca_bv, L1_xattn_ca_wo, L1_xattn_ca_bo, L1_xattn_ffn_w1, L1_xattn_ffn_b1, L1_xattn_ffn_w2, L1_xattn_ffn_b2, L1_xattn_ln1_g, L1_xattn_ln1_b, L1_xattn_ln2_g, L1_xattn_ln2_b, L1_xattn_ln3_g, L1_xattn_ln3_b)
    return x

_drawn_inputs = setup_inputs


def setup_inputs(seed=0):
    import zlib

    import numpy as np

    out = dict(_drawn_inputs(seed))
    spreads = {'L0_xattn_norm_w': (1.0, 0.6),
     'L1_xattn_sa_bq': (0.0, 0.8),
     'L1_xattn_sa_bk': (0.0, 0.8),
     'L1_xattn_sa_bv': (0.0, 0.1),
     'L1_xattn_sa_bo': (0.0, 0.1),
     'L1_xattn_ca_bq': (0.0, 0.8),
     'L1_xattn_ca_bk': (0.0, 0.8),
     'L1_xattn_ca_bv': (0.0, 0.1),
     'L1_xattn_ca_bo': (0.0, 0.1),
     'L1_xattn_ffn_b1': (0.0, 0.1),
     'L1_xattn_ffn_b2': (0.0, 0.1),
     'L1_xattn_ln1_g': (1.0, 0.2),
     'L1_xattn_ln1_b': (0.0, 0.1),
     'L1_xattn_ln2_g': (1.0, 0.2),
     'L1_xattn_ln2_b': (0.0, 0.1),
     'L1_xattn_ln3_g': (1.0, 0.2),
     'L1_xattn_ln3_b': (0.0, 0.1)}
    factors = {'L1_xattn_sa_wq': 8.0,
     'L1_xattn_sa_wk': 8.0,
     'L1_xattn_ca_wq': 7.683,
     'L1_xattn_ca_wk': 7.491}
    for name, (base, spread) in spreads.items():
        noise = np.random.default_rng([zlib.crc32(name.encode()), seed]).standard_normal(out[name].shape)
        drawn = base * np.exp(spread * noise) if base else spread * noise
        out[name] = jnp.asarray(drawn.astype(out[name].dtype))
    for name, factor in factors.items():
        out[name] = (out[name] * factor).astype(out[name].dtype)
    return out
```

```python
from contextlib import ExitStack

import concourse.bass as bass
from concourse import mybir

ALU = mybir.AluOpType
ACT = mybir.ActivationFunctionType
AX = mybir.AxisListType
F32 = mybir.dt.float32
F32R = mybir.dt.float32r
I32 = mybir.dt.int32

P = 128
D = 512
S = 256
H = 16
KC = D // P
TB = S // P
UF = 256
CU = UF // P
RMS_EPS = 1e-6
LN_EPS = 1e-5
MASKED = -1e30
RSQRT_SEED = float(0x5F3759DF)
RSQRT_STEPS = 3
RSQRT_OPS = 1 + 3 * RSQRT_STEPS

PARTS = ((0, 0), (0, 1), (1, 0))


def matmul3(pe, out, lhs, rhs, first, last):
    for n, (a, b) in enumerate(PARTS):
        mm = pe.matmul(out, lhs[a], rhs[b], start=first and n == 0, stop=last and n == 2)
    return mm


def rsqrt_ops(dve, v, r, t, chain):
    chain(dve.tensor_scalar(r.bitcast(I32), v.bitcast(I32), -0.5, RSQRT_SEED, ALU.mult, ALU.add))
    for _ in range(RSQRT_STEPS):
        chain(dve.scalar_tensor_tensor(out=t, in0=v, scalar=-0.5, in1=r, op0=ALU.mult, op1=ALU.mult))
        chain(dve.tensor_tensor(t, t, r, ALU.mult))
        chain(dve.scalar_tensor_tensor(out=r, in0=t, scalar=1.5, in1=r, op0=ALU.add, op1=ALU.mult))


def make_identity(pool, ident, s_ident):
    pool.memset(ident[:, :], 0.0).then_inc(s_ident, 1)
    pool.wait_ge(s_ident, 1)
    pool.affine_select(out=ident[:, :], in_=ident[:, :], compare_op=ALU.not_equal, fill=1.0,
                       base=0, pattern=[[-1, P]], channel_multiplier=1).then_inc(s_ident, 1)


LN_CHAIN = 2 * TB + 1 + RSQRT_OPS + TB + 1


def layernorm_ops(dve, y, yo, stats, mv, ve, rs, tmp, g, b, chain):
    for t in range(TB):
        chain(dve.bn_stats(stats[:, t, :], y[:, t, :]))
        dve.nop(nofuse=True)
        chain(dve.bn_aggr(mv[:, t, :], stats[:, t, :]))
    chain(dve.tensor_scalar(ve[:, :], mv[:, :, 1], LN_EPS, None, ALU.add))
    rsqrt_ops(dve, ve[:, :], rs[:, :], tmp[:, :], chain)
    for t in range(TB):
        chain(dve.tensor_scalar(yo[:, t, :], y[:, t, :], mv[:, t, 0:1], rs[:, t:t + 1], ALU.subtract, ALU.mult))
    chain(dve.tensor_tensor(yo[:, :, :], yo[:, :, :], g[:, :].unsqueeze(1).to_broadcast([P, TB, D]), ALU.mult))
    return dve.tensor_tensor(yo[:, :, :], yo[:, :, :], b[:, :].unsqueeze(1).to_broadcast([P, TB, D]), ALU.add)


def attention_phase(nc, tag, B, src, kv, w, dst, d, norm_w=None, bias=None, mask=None, ln=None):
    DI = H * d
    U = DI // UF
    HU = UF // d
    assert U % 2 == 0 and B >= 3
    self_attention = kv is None
    transposed_weights = norm_w is None
    WQ, WK, WV, WO = (n * KC * DI for n in range(4))
    NW = 4 * KC * DI

    with ExitStack() as ctx:
        def sb(name, shape, dt):
            return ctx.enter_context(nc.sbuf_tensor(tag + name, shape, dt))

        def ps(name):
            return ctx.enter_context(nc.psum_tensor(tag + name, [P, 512], F32))

        def sem(name):
            return ctx.enter_context(nc.semaphore(tag + name))

        def pair(name, shape):
            return sb(name + "_hi", shape, F32R), sb(name + "_lo", shape, F32R)

        W = pair("w", [P, NW])
        xT = pair("xT", [P, KC, S])
        cT = xT if self_attention else pair("cT", [P, KC, S])
        q = pair("q", [P, 2, CU, S])
        k = pair("k", [P, 2, CU, S])
        v = sb("v", [P, 2, TB, HU, 2 * d], F32R)
        pT = pair("pT", [P, 2, TB, S])
        oT = pair("oT", [P, CU, S])
        x_raw = sb("x_raw", [P, TB, D], F32)
        c_raw = sb("c_raw", [P, TB, D], F32)
        y = sb("y", [P, TB, D], F32)
        yo = sb("yo", [P, TB, D], F32)
        probs = sb("probs", [P, 2, TB, S], F32)
        o = sb("o", [P, TB, UF], F32)
        ident = sb("ident", [P, P], F32)
        neg_max = sb("neg_max", [P, 2, TB], F32)
        row_sum = sb("row_sum", [P, 2, TB, HU], F32)
        inv_sum = sb("inv_sum", [P, TB, HU], F32)
        if norm_w is not None:
            nw = sb("nw", [P, KC], F32)
            raw_max = sb("raw_max", [P, 2, TB], F32)
            squares = sb("squares", [P, D], F32)
            sumsq = sb("sumsq", [P, TB], F32)
            rstd_next = sb("rstd_next", [P, TB], F32)
            rstd = sb("rstd", [P, TB], F32)
            rtmp = sb("rtmp", [P, TB], F32)
        if mask is not None:
            mask_raw = sb("mask_raw", [P, TB, S], I32)
            mask_add = sb("mask_add", [P, TB, S], F32)
        if bias is not None:
            bqk = sb("bqk", [P, 2, KC], F32)
            bo = sb("bo", [P, D], F32)
            bv_raw = sb("bv_raw", [1, D], F32)
            bv = sb("bv_hi", [1, D], F32R), sb("bv_lo", [1, D], F32R)
            ones_f = sb("ones_f", [1, P], F32)
            ones = sb("ones", [1, P], F32R)
        if ln is not None:
            ln_g = sb("ln_g", [P, D], F32)
            ln_b = sb("ln_b", [P, D], F32)
            stats = sb("stats", [P, TB, 6], F32)
            mv = sb("mv", [P, TB, 2], F32)
            ve = sb("ve", [P, TB], F32)
            rs = sb("rs", [P, TB], F32)
            ntmp = sb("ntmp", [P, TB], F32)

        scores_ps = [ps("scores0"), ps("scores1")]
        probsT_ps = [ps("probsT0"), ps("probsT1")]
        out_ps = [ps("out0"), ps("out1")]
        job_ps = [ps("job0"), ps("job1")]

        s_x = sem("s_x")
        s_m = sem("s_m")
        s_small = sem("s_small")
        s_w = [sem("s_w0"), sem("s_w1")]
        s_ident = sem("s_ident")
        s_whi = sem("s_whi")
        s_wlo = sem("s_wlo")
        s_bv = sem("s_bv")
        s_job = sem("s_job")
        s_job_hi = sem("s_job_hi")
        s_job_done = sem("s_job_done")
        s_scores = sem("s_scores")
        s_rawmax = sem("s_rawmax")
        s_max = sem("s_max")
        s_exp = sem("s_exp")
        s_probsT = sem("s_probsT")
        s_pT_hi = sem("s_pT_hi")
        s_pT_lo = sem("s_pT_lo")
        s_pv = sem("s_pv")
        s_osum = sem("s_osum")
        s_o = sem("s_o")
        s_mask = sem("s_mask")
        s_rms = sem("s_rms")
        s_rstd = sem("s_rstd")
        s_yinit = sem("s_yinit")
        s_ln = sem("s_ln")
        s_fin = sem("s_fin")
        s_store = sem("s_store")

        def jobs(u, step, prev1=True, prev2=True, nxt=True):
            at = dict(wo0=0, wo1=0, T=1, q=1, k=2, o=2, v=3) if HU == 4 else \
                dict(wo0=0, wo1=1, T=2, q=3, k=4, o=5, v=6)
            un = (u + 1) % U
            out = []
            if prev2:
                out += [("wo", (t, (u - 2) % U)) for t in range(TB) if at[f"wo{t}"] == step]
            if nxt and u == U - 1 and at["T"] == step:
                out += load_jobs()
            if nxt and at["q"] == step:
                out.append(("q", un))
            if nxt and at["k"] == step:
                out.append(("k", un))
            if prev1 and at["o"] == step:
                out.append(("o", None))
            if nxt and at["v"] == step:
                out.append(("v", un))
            return out

        def load_jobs():
            return ([] if self_attention else [("cT", 0), ("cT", 1)]) + [("xT", 0), ("xT", 1)]

        def exist(seg, u):
            first, last = seg == "first", seg == "last"
            return dict(prev1=not (first and u == 0), prev2=not (first and u < 2), nxt=not (last and u == U - 1))

        def seg_jobs(seg):
            return [j for u in range(U) for st in range(HU) for j in jobs(u, st, **exist(seg, u))]

        weight_jobs = [("wT", (n, r)) for n in range(4) for r in range(D // P)] if transposed_weights else []
        pro_jobs = weight_jobs + load_jobs() + [("q", 0), ("k", 0), ("v", 0)]
        epi_jobs = [("wo", (0, U - 2)), ("wo", (1, U - 2)), ("o", None), ("wo", (0, U - 1)), ("wo", (1, U - 1))]

        def has_hi(kind):
            return kind != "wo"

        def counts(js):
            return len(js), sum(has_hi(kind) for kind, _ in js)

        N_PRO, N_FIRST, N_MID, N_LAST = (counts(x) for x in
                                         (pro_jobs, seg_jobs("first"), seg_jobs("mid"), seg_jobs("last")))
        assert N_MID[0] % 2 == 0

        class Place:

            def __init__(self, b, all_jobs, hi_jobs, parity, prev=None):
                self.b, self.base, self.hi_base, self.parity, self.prev = b, all_jobs, hi_jobs, parity, prev
                self.n = self.n_hi = self.slot_start = 0

            def next(self, kind):
                bank = job_ps[(self.parity + self.n) % 2]
                self.n += 1
                self.n_hi += has_hi(kind)
                self.prev = kind
                return bank

            @property
            def job(self):
                return self.base + self.n

            @property
            def hi_job(self):
                return self.hi_base + self.n_hi

        def run(eng, prologue, step, epilogue):
            def entry(seg, place):
                for u in range(U):
                    for st in range(HU):
                        step(place, seg, u, st)

            prologue(Place(None, 0, 0, 0))
            entry("first", Place(0, N_PRO[0], N_PRO[1], N_PRO[0]))
            b0 = tuple(N_PRO[n] + N_FIRST[n] for n in range(2))
            with eng.Fori(1, B - 1) as b:
                entry("mid", Place(b, (b - 1) * N_MID[0] + b0[0], (b - 1) * N_MID[1] + b0[1], b0[0]))
            b1 = tuple(b0[n] + (B - 2) * N_MID[n] for n in range(2))
            entry("last", Place(B - 1, b1[0], b1[1], b1[0]))
            e = tuple(b1[n] + N_LAST[n] for n in range(2))
            epilogue(Place(B, e[0], e[1], e[0], prev="o"))

        def head_wait(eng, s, seg, place, h, lag, count):
            if seg == "first" and h - lag + 1 <= 0:
                return
            eng.wait_ge(s, place.b * H + (h - lag + 1) if count is None else count)

        def unit_count(place, u):
            return place.b * U + (u + 1)

        def wT_out(part, n, r):
            return W[part][:, n * KC * D:(n + 1) * KC * D].rearrange("p (c f) -> p c f", c=KC)[:, :, r * P:(r + 1) * P]

        stage = [y, yo]
        L0_PIECES = NW // (TB * D)

        block = ctx.enter_context(nc.Block())

        @block.sync
        def _(sp):
            x_v = src.rearrange("b (t p) f -> b p t f", p=P)
            dst_v = dst.rearrange("b (t p) f -> b p t f", p=P)

            def load(b):
                sp.dma_start(x_raw[:, :, :], x_v[b]).then_inc(s_x, 16)
                if not self_attention:
                    sp.dma_start(c_raw[:, :, :], kv.rearrange("b (t p) f -> b p t f", p=P)[b]).then_inc(s_x, 16)
                if mask is not None:
                    if mask.shape[2] == 1:
                        sp.dma_start(mask_raw[:, 0, :], mask[b, 0, 0].partition_broadcast(P)).then_inc(s_m, 16)
                        sp.dma_start(mask_raw[:, 1, :], mask[b, 0, 0].partition_broadcast(P)).then_inc(s_m, 16)
                    else:
                        m_v = mask.rearrange("b a (t p) k -> (b a) p t k", p=P)
                        sp.dma_start(mask_raw[:, :, :], m_v[b]).then_inc(s_m, 16)

            def store(b):
                sp.wait_ge(s_fin, b + 1)
                sp.dma_start(dst_v[b], yo[:, :, :]).then_inc(s_store, 16)

            if norm_w is not None:
                with nc.allow_non_contiguous_dma("a column per chunk"):
                    sp.dma_start(nw[:, :], norm_w.rearrange("(c p) -> p c", p=P)).then_inc(s_small, 16)
            if bias is not None:
                with nc.allow_non_contiguous_dma("a column per chunk"):
                    sp.dma_start(bqk[:, 0, :], bias[0].rearrange("(c p) -> p c", p=P)).then_inc(s_small, 16)
                    sp.dma_start(bqk[:, 1, :], bias[1].rearrange("(c p) -> p c", p=P)).then_inc(s_small, 16)
                sp.dma_start(bv_raw[:, :], bias[2].rearrange("(a f) -> a f", a=1)).then_inc(s_small, 16)
                sp.dma_start(bo[:, :], bias[3].partition_broadcast(P)).then_inc(s_small, 16)
                sp.dma_start(ln_g[:, :], ln[0].partition_broadcast(P)).then_inc(s_small, 16)
                sp.dma_start(ln_b[:, :], ln[1].partition_broadcast(P)).then_inc(s_small, 16)
            if transposed_weights:
                for i in range(4 * D // (TB * P)):
                    if i >= 2:
                        sp.wait_ge(s_job, TB * (i - 1))
                    n, half = i // 2, i % 2
                    sp.dma_start(stage[i % 2][:, :, :], w[n][half * S:(half + 1) * S, :].rearrange(
                        "(t p) f -> p t f", p=P)).then_inc(s_w[i % 2], 16)
            else:
                for i in range(L0_PIECES):
                    if i >= 2:
                        sp.wait_ge(s_wlo, i - 1)
                    if i < 3 * KC:
                        piece = w[i // KC][(i % KC) * P:(i % KC + 1) * P, :].rearrange("p (t f) -> p t f", t=TB)
                    else:
                        r = (i - 3 * KC) * TB * P
                        piece = w[3][r:r + TB * P, :].rearrange("(t p) f -> p t f", p=P)
                    sp.dma_start(stage[i % 2][:, :, :], piece).then_inc(s_w[i % 2], 16)
            load(0)
            sp.wait_ge(s_yinit, 1)
            load(1)
            with sp.Fori(1, B - 1) as b:
                store(b - 1)
                sp.wait_ge(s_yinit, b + 1)
                load(b + 1)
            store(B - 2)
            store(B - 1)
            sp.wait_ge(s_store, 16 * B)

        @block.gpsimd
        def _(pool):
            make_identity(pool, ident, s_ident)

        @block.tensor
        def _(pe):
            def transposes(bank, tiles):
                for n, t in enumerate(tiles):
                    tr = pe.transpose(bank[:, n * P:(n + 1) * P], t, ident[:, :])
                return tr

            def job(place, kind, arg):
                n, prev = place.job, place.prev
                bank = place.next(kind)
                if (kind, prev) in (("q", "xT"), ("wo", "o")):
                    pe.wait_ge(s_job_done, n)
                elif place.b is not None or n >= 2:
                    pe.wait_ge(s_job_done, n - 1)
                if kind == "wT":
                    wi, r = arg
                    i = wi * 2 + r // 2
                    if r % 2 == 0:
                        pe.wait_ge(s_w[i % 2], 16 * (i // 2 + 1))
                    mm = transposes(bank, [stage[i % 2][:, r % 2, c * P:(c + 1) * P] for c in range(KC)])
                elif kind in ("xT", "cT"):
                    raw = x_raw if kind == "xT" else c_raw
                    nb = 0 if place.b is None else place.b + 1
                    pe.wait_ge(s_x, (nb + 1) * (16 if self_attention else 32))
                    mm = transposes(bank, [raw[:, t, c * P:(c + 1) * P] for c in (2 * arg, 2 * arg + 1)
                                           for t in range(TB)])
                elif kind in ("q", "k"):
                    a = xT if kind == "q" else cT
                    off = WQ if kind == "q" else WK
                    for c in range(CU):
                        for kc in range(KC):
                            f = off + kc * DI + arg * UF + c * P
                            mm = matmul3(pe, bank[:, c * S:(c + 1) * S], [x[:, f:f + P] for x in W],
                                         [x[:, kc, :] for x in a], kc == 0, kc == KC - 1)
                elif kind == "v":
                    for t in range(TB):
                        out = bank[:, t * UF:(t + 1) * UF]
                        for kc in range(KC):
                            f = WV + kc * DI + arg * UF
                            mm = matmul3(pe, out, [x[:, kc, t * P:(t + 1) * P] for x in cT],
                                         [x[:, f:f + UF] for x in W], kc == 0, kc == KC - 1 and bias is None)
                        if bias is not None:
                            pe.matmul(out, ones[:, :], bv[0][:, arg * UF:(arg + 1) * UF], start=False, stop=False)
                            mm = pe.matmul(out, ones[:, :], bv[1][:, arg * UF:(arg + 1) * UF], start=False, stop=True)
                elif kind == "o":
                    pe.wait_ge(s_o, unit_count(place, arg))
                    mm = transposes(bank, [o[:, t, c * P:(c + 1) * P] for c in range(CU) for t in range(TB)])
                else:
                    t, u = arg
                    for c in range(CU):
                        f = WO + (u * CU + c) * D
                        mm = matmul3(pe, bank[:, :], [x[:, c, t * P:(t + 1) * P] for x in oT],
                                     [x[:, f:f + D] for x in W], c == 0, c == CU - 1)
                mm.then_inc(s_job, 1)

            def scores(place, seg, u, j):
                h = u * HU + j
                if j == 0:
                    pe.wait_ge(s_job_done, place.job - 1)
                head_wait(pe, s_exp, seg, place, h, 2, None)
                bank = scores_ps[h % 2]
                c, r = j * d // P, j * d % P
                for t in range(TB):
                    mm = matmul3(pe, bank[:, t * S:(t + 1) * S],
                                 [x[r:r + d, u % 2, c, t * P:(t + 1) * P] for x in q],
                                 [x[r:r + d, u % 2, c, :] for x in k], True, True)
                mm.then_inc(s_scores, 1)

            def transpose_probs(place, seg, h):
                head_wait(pe, s_exp, seg, place, h, 0, None)
                head_wait(pe, s_pT_lo, seg, place, h, 2, None)
                hb = h % 2
                transposes(probsT_ps[hb], [probs[:, hb, t, kb * P:(kb + 1) * P] for kb in range(TB)
                                           for t in range(TB)]).then_inc(s_probsT, 1)

            def attend(place, seg, h, v_jobs):
                j, ub = h % HU, (h // HU) % 2
                if j == 0:
                    pe.wait_ge(s_job_done, v_jobs)
                    n = unit_count(place, h // HU) - 1
                    if not (seg == "first" and h < HU):
                        pe.wait_ge(s_osum, 3 * n)
                head_wait(pe, s_pT_lo, seg, place, h, 0, None)
                hb = h % 2
                for t in range(TB):
                    for n, (kb, part) in enumerate([(a, b) for a in range(TB) for b in range(2)]):
                        mm = pe.matmul(out_ps[t][:, j * 2 * d:(j + 1) * 2 * d],
                                       pT[part][:, hb, kb, t * P:(t + 1) * P], v[:, ub, kb, j, :],
                                       start=n == 0, stop=n == 2 * TB - 1)
                mm.then_inc(s_pv, 1)

            def prologue(place):
                pe.wait_ge(s_ident, 2)
                if bias is not None:
                    pe.wait_ge(s_bv, 4)
                if not transposed_weights:
                    pe.wait_ge(s_wlo, L0_PIECES)
                for kind, arg in pro_jobs:
                    job(place, kind, arg)

            def step(place, seg, u, j):
                h = u * HU + j
                if j == 0:
                    place.slot_start = place.job
                scores(place, seg, u, j)
                if h >= 1 or seg != "first":
                    transpose_probs(place, seg, h - 1)
                if h >= 2 or seg != "first":
                    attend(place, seg, h - 2, place.slot_start)
                for kind, arg in jobs(u, j, **exist(seg, u)):
                    job(place, kind, u - 1 if kind == "o" else arg)

            def epilogue(place):
                transpose_probs(place, "epi", -1)
                attend(place, "epi", -2, None)
                attend(place, "epi", -1, None)
                for kind, arg in epi_jobs:
                    job(place, kind, -1 if kind == "o" else arg)

            run(pe, prologue, step, epilogue)

        @block.scalar
        def _(act):
            def job(place, kind, arg):
                bank = place.next(kind)
                if not has_hi(kind):
                    return
                act.wait_ge(s_job, place.job)
                if kind == "wT":
                    hi = act.activation(wT_out(0, *arg), bank[:, :].rearrange("p (c f) -> p c f", c=KC), ACT.Copy)
                elif kind in ("xT", "cT"):
                    a = xT if kind == "xT" else cT
                    hi = act.activation(a[0][:, 2 * arg:2 * arg + 2, :],
                                        bank[:, :].rearrange("p (c t) -> p c t", c=2), ACT.Copy)
                elif kind in ("q", "k"):
                    out = (q if kind == "q" else k)[0][:, arg % 2, :, :]
                    if bias is None:
                        hi = act.activation(out, bank[:, :].rearrange("p (c t) -> p c t", c=CU), ACT.Copy)
                    else:
                        for c in range(CU):
                            b_col = bqk[:, int(kind == "k"), arg * CU + c:arg * CU + c + 1]
                            hi = act.activation(out[:, c, :], bank[:, c * S:(c + 1) * S], ACT.Identity, bias=b_col)
                elif kind == "v":
                    hi = act.activation(v[:, arg % 2, :, :, 0:d],
                                        bank[:, :].rearrange("p (t h e) -> p t h e", t=TB, h=HU), ACT.Copy)
                else:
                    hi = act.activation(oT[0][:, :, :], bank[:, :].rearrange("p (c t) -> p c t", c=CU), ACT.Copy)
                hi.then_inc(s_job_hi, 1)

            def exps(place, seg, u, j):
                h = u * HU + j
                head_wait(act, s_max, seg, place, h, 0, None)
                head_wait(act, s_probsT, seg, place, h, 2, None)
                if j == 0 and not (seg == "first" and u < 2):
                    act.wait_ge(s_o, unit_count(place, u - 2))
                for t in range(TB):
                    scale = rstd[:, t:t + 1] if norm_w is not None else -1.0
                    e = act.activation(probs[:, h % 2, t, :], scores_ps[h % 2][:, t * S:(t + 1) * S], ACT.Exp,
                                       bias=neg_max[:, h % 2, t:t + 1], scale=scale,
                                       accum_out=row_sum[:, u % 2, t, j:j + 1])
                e.then_inc(s_exp, 1)

            def probsT_hi(place, seg, h):
                head_wait(act, s_probsT, seg, place, h, 0, None)
                head_wait(act, s_pv, seg, place, h, 2, None)
                act.activation(pT[0][:, h % 2, :, :], probsT_ps[h % 2][:, :].rearrange("p (k t) -> p k t", k=TB),
                               ACT.Copy).then_inc(s_pT_hi, 1)

            def prologue(place):
                if bias is not None:
                    act.wait_ge(s_bv, 1)
                    act.wait_ge(s_small, 16 * 6)
                    act.activation(ones[:, :], ones_f[:, :], ACT.Copy).then_inc(s_bv, 1)
                    act.activation(bv[0][:, :], bv_raw[:, :], ACT.Copy).then_inc(s_bv, 1)
                if not transposed_weights:
                    act.wait_ge(s_small, 16)
                    for i in range(L0_PIECES):
                        act.wait_ge(s_w[i % 2], 16 * (i // 2 + 1))
                        scale = nw[:, i:i + 1] if i < KC else 1.0
                        act.activation(W[0][:, i * TB * D:(i + 1) * TB * D],
                                       stage[i % 2][:, :, :].rearrange("p t f -> p (t f)"), ACT.Copy,
                                       scale=scale).then_inc(s_whi, 1)
                for kind, arg in pro_jobs:
                    job(place, kind, arg)

            def step(place, seg, u, j):
                h = u * HU + j
                if h >= 1 or seg != "first":
                    probsT_hi(place, seg, h - 1)
                exps(place, seg, u, j)
                for kind, arg in jobs(u, j, **exist(seg, u)):
                    job(place, kind, arg)

            def epilogue(place):
                probsT_hi(place, "epi", -1)
                for kind, arg in epi_jobs:
                    job(place, kind, arg)

            run(act, prologue, step, epilogue)

        @block.vector
        def _(dve):
            def job(place, kind, arg):
                n = place.job
                bank = place.next(kind)
                if has_hi(kind):
                    dve.wait_ge(s_job_hi, place.hi_job)
                if kind == "wT":
                    lo = dve.tensor_tensor(wT_out(1, *arg), bank[:, :].rearrange("p (c f) -> p c f", c=KC),
                                           wT_out(0, *arg), ALU.subtract)
                elif kind in ("xT", "cT"):
                    a = xT if kind == "xT" else cT
                    sl = slice(2 * arg, 2 * arg + 2)
                    lo = dve.tensor_tensor(a[1][:, sl, :], bank[:, :].rearrange("p (c t) -> p c t", c=2),
                                           a[0][:, sl, :], ALU.subtract)
                elif kind in ("q", "k"):
                    a = q if kind == "q" else k
                    hi, out = a[0][:, arg % 2, :, :], a[1][:, arg % 2, :, :]
                    if bias is None:
                        lo = dve.tensor_tensor(out, bank[:, :].rearrange("p (c t) -> p c t", c=CU), hi, ALU.subtract)
                    else:
                        for c in range(CU):
                            b_col = bqk[:, int(kind == "k"), arg * CU + c:arg * CU + c + 1]
                            lo = dve.scalar_tensor_tensor(out=out[:, c, :], in0=bank[:, c * S:(c + 1) * S],
                                                          scalar=b_col, in1=hi[:, c, :], op0=ALU.add,
                                                          op1=ALU.subtract)
                elif kind == "v":
                    lo = dve.tensor_tensor(v[:, arg % 2, :, :, d:2 * d],
                                           bank[:, :].rearrange("p (t h e) -> p t h e", t=TB, h=HU),
                                           v[:, arg % 2, :, :, 0:d], ALU.subtract)
                elif kind == "o":
                    lo = dve.tensor_tensor(oT[1][:, :, :], bank[:, :].rearrange("p (c t) -> p c t", c=CU),
                                           oT[0][:, :, :], ALU.subtract)
                else:
                    t = arg[0]
                    dve.wait_ge(s_job, place.job)
                    dve.wait_ge(s_job_done, n)
                    lo = dve.tensor_tensor(y[:, t, :], y[:, t, :], bank[:, :], ALU.add)
                lo.then_inc(s_job_done, 1)

            def chain_on(s, base):
                done = [0]

                def chain(ins):
                    done[0] += 1
                    ins.then_inc(s, 1)
                    dve.wait_ge(s, base + done[0])
                return chain

            def rstd_of_next(nb):
                chain = chain_on(s_rms, nb * (TB + RSQRT_OPS))
                dve.wait_ge(s_x, (nb + 1) * 32)
                for t in range(TB):
                    chain(dve.tensor_tensor_reduce(out=squares[:, :], in0=x_raw[:, t, :], in1=x_raw[:, t, :],
                                                   scale=1.0 / D, scalar=RMS_EPS, op0=ALU.mult, op1=ALU.add,
                                                   accum_out=sumsq[:, t:t + 1]))
                rsqrt_ops(dve, sumsq[:, :], rstd_next[:, :], rtmp[:, :], chain)

            def maxima(place, seg, u, j):
                h = u * HU + j
                hb = h % 2
                if h == 0:
                    if norm_w is not None:
                        if seg != "first":
                            dve.wait_ge(s_exp, place.b * H)
                        dve.tensor_copy(rstd[:, :], rstd_next[:, :]).then_inc(s_rstd, 1)
                        dve.wait_ge(s_rstd, place.b + 1)
                    if mask is not None:
                        if seg != "first":
                            dve.wait_ge(s_max, place.b * H)
                        dve.wait_ge(s_m, (place.b + 1) * (32 if mask.shape[2] == 1 else 16))
                        dve.tensor_scalar(mask_add[:, :, :], mask_raw[:, :, :], 0.0, MASKED, ALU.is_equal,
                                          ALU.mult).then_inc(s_mask, 1)
                        dve.wait_ge(s_mask, place.b + 1)
                head_wait(dve, s_scores, seg, place, h, 0, None)
                bank = scores_ps[hb]
                if norm_w is not None:
                    dve.tensor_reduce(raw_max[:, hb, :], bank[:, :].rearrange("p (t k) -> p t k", t=TB), AX.X,
                                      ALU.max, negate=True).then_inc(s_rawmax, 1)
                    head_wait(dve, s_rawmax, seg, place, h, 0, None)
                    dve.tensor_tensor(neg_max[:, hb, :], raw_max[:, hb, :], rstd[:, :],
                                      ALU.mult).then_inc(s_max, 1)
                else:
                    dve.nop(nofuse=True)
                    for t in range(TB):
                        m = dve.tensor_tensor_reduce(out=bank[:, t * S:(t + 1) * S], in0=bank[:, t * S:(t + 1) * S],
                                                     in1=mask_add[:, t, :], scale=-float(d) ** -0.5, scalar=3e38,
                                                     op0=ALU.add, op1=ALU.min, accum_out=neg_max[:, hb, t:t + 1])
                    m.then_inc(s_max, 1)

            def probsT_lo(place, seg, h):
                head_wait(dve, s_pT_hi, seg, place, h, 0, None)
                hb = h % 2
                dve.tensor_tensor(pT[1][:, hb, :, :], probsT_ps[hb][:, :].rearrange("p (k t) -> p k t", k=TB),
                                  pT[0][:, hb, :, :], ALU.subtract).then_inc(s_pT_lo, 1)

            def unit_output(place, u):
                n = unit_count(place, u)
                base = (n - 1) * 3
                chain = chain_on(s_osum, base)
                dve.wait_ge(s_pv, n * HU)
                if not (isinstance(n, int) and n == 1):
                    dve.wait_ge(s_job, place.job)
                chain(dve.reciprocal(inv_sum[:, :, :], row_sum[:, u % 2, :, :]))
                for t in range(TB):
                    chain(dve.tensor_reduce(o[:, t, :].rearrange("p (h e) -> p h e", h=HU),
                                            out_ps[t][:, :].rearrange("p (h n e) -> p h e n", h=HU, n=2),
                                            AX.X, ALU.add))
                out = o[:, :, :].rearrange("p t (h e) -> p t h e", h=HU)
                dve.tensor_tensor(out, out, inv_sum[:, :, :].unsqueeze(3).to_broadcast([P, TB, HU, d]),
                                  ALU.mult).then_inc(s_o, 1)

            def finish(place, b):
                if not (isinstance(b, int) and b == 0):
                    dve.wait_ge(s_store, 16 * b)
                dve.wait_ge(s_job_done, place.job)
                if ln is None:
                    dve.tensor_copy(yo[:, :, :], y[:, :, :]).then_inc(s_fin, 1)
                else:
                    layernorm_ops(dve, y, yo, stats, mv, ve, rs, ntmp, ln_g, ln_b,
                                  chain_on(s_ln, b * LN_CHAIN)).then_inc(s_fin, 1)

            def residual(place):
                if isinstance(place.b, int) and place.b == 0:
                    pass
                else:
                    dve.wait_ge(s_fin, place.b)
                if bias is None:
                    dve.tensor_copy(y[:, :, :], x_raw[:, :, :]).then_inc(s_yinit, 1)
                else:
                    dve.tensor_tensor(y[:, :, :], x_raw[:, :, :],
                                      bo[:, :].unsqueeze(1).to_broadcast([P, TB, D]), ALU.add).then_inc(s_yinit, 1)
                dve.wait_ge(s_yinit, place.b + 1)

            def prologue(place):
                if bias is not None:
                    dve.memset(ones_f[:, :], 1.0).then_inc(s_bv, 1)
                    dve.wait_ge(s_bv, 3)
                    dve.wait_ge(s_small, 16 * 6)
                    dve.tensor_tensor(bv[1][:, :], bv_raw[:, :], bv[0][:, :], ALU.subtract).then_inc(s_bv, 1)
                if not transposed_weights:
                    dve.wait_ge(s_small, 16)
                    for i in range(L0_PIECES):
                        dve.wait_ge(s_w[i % 2], 16 * (i // 2 + 1))
                        dve.wait_ge(s_whi, i + 1)
                        cols = slice(i * TB * D, (i + 1) * TB * D)
                        raw = stage[i % 2][:, :, :].rearrange("p t f -> p (t f)")
                        if i < KC:
                            lo = dve.scalar_tensor_tensor(out=W[1][:, cols], in0=raw, scalar=nw[:, i:i + 1],
                                                          in1=W[0][:, cols], op0=ALU.mult, op1=ALU.subtract)
                        else:
                            lo = dve.tensor_tensor(W[1][:, cols], raw, W[0][:, cols], ALU.subtract)
                        lo.then_inc(s_wlo, 1)
                    rstd_of_next(0)
                for kind, arg in pro_jobs:
                    job(place, kind, arg)

            def step(place, seg, u, j):
                h = u * HU + j
                if j == 2 and (u >= 1 or seg != "first"):
                    unit_output(place, u - 1)
                maxima(place, seg, u, j)
                if h >= 1 or seg != "first":
                    probsT_lo(place, seg, h - 1)
                for kind, arg in jobs(u, j, **exist(seg, u)):
                    job(place, kind, arg)
                if u == 1 and j == (0 if HU == 4 else 1):
                    if seg != "first":
                        finish(place, place.b - 1)
                    residual(place)
                if norm_w is not None and u == U - 1 and j == HU - 1 and seg != "last":
                    rstd_of_next(place.b + 1)

            def epilogue(place):
                probsT_lo(place, "epi", -1)
                unit_output(place, -1)
                for kind, arg in epi_jobs:
                    job(place, kind, arg)
                finish(place, B - 1)

            run(dve, prologue, step, epilogue)


def ffn_phase(nc, tag, B, src, w1, b1, w2, b2, ln, dst):
    F = w1.shape[0]
    FC = F // P
    HJ = FC // 2
    W1N, W2N = KC * F, FC * D
    assert B >= 3

    with ExitStack() as ctx:
        def sb(name, shape, dt):
            return ctx.enter_context(nc.sbuf_tensor(tag + name, shape, dt))

        def sem(name):
            return ctx.enter_context(nc.semaphore(tag + name))

        def pair(name, shape):
            return sb(name + "_hi", shape, F32R), sb(name + "_lo", shape, F32R)

        w1T = pair("w1T", [P, KC, F])
        w2T = pair("w2T", [P, FC, D])
        xT = pair("xT", [P, KC, S])
        hT = pair("hT", [P, FC, S])
        hidden = sb("hidden", [P, 2, 2, S], F32)
        x_raw = sb("x_raw", [P, TB, D], F32)
        y = sb("y", [P, TB, D], F32)
        yo = sb("yo", [P, TB, D], F32)
        ident = sb("ident", [P, P], F32)
        b1c = sb("b1c", [P, FC], F32)
        b2b = sb("b2b", [P, D], F32)
        ln_g = sb("ln_g", [P, D], F32)
        ln_b = sb("ln_b", [P, D], F32)
        stats = sb("stats", [P, TB, 6], F32)
        mv = sb("mv", [P, TB, 2], F32)
        ve = sb("ve", [P, TB], F32)
        rs = sb("rs", [P, TB], F32)
        ntmp = sb("ntmp", [P, TB], F32)
        job_ps = [ctx.enter_context(nc.psum_tensor(f"{tag}job{n}", [P, 512], F32)) for n in range(2)]

        s_ident = sem("s_ident")
        s_small = sem("s_small")
        s_w = [sem("s_w0"), sem("s_w1")]
        s_x = sem("s_x")
        s_job = sem("s_job")
        s_job_hi = sem("s_job_hi")
        s_job_done = sem("s_job_done")
        s_split = sem("s_split")
        s_yinit = sem("s_yinit")
        s_ln = sem("s_ln")
        s_fin = sem("s_fin")
        s_store = sem("s_store")

        stage = [y, yo]
        W_JOBS = [("w1T", r) for r in range(FC)] + [("w2T", (r, g)) for r in range(D // P) for g in range(KC)]
        PRO = W_JOBS + [("xT", 0), ("xT", 1)]

        def entry_jobs(last):
            return [("h", n) for n in range(HJ)] + ([] if last else [("xT", 0), ("xT", 1)]) + [("y", 0), ("y", 1)]

        N = len(entry_jobs(False))
        assert N % 2 == 0 and len(PRO) % 2 == 0

        N_HI = sum(kind != "y" for kind, _ in entry_jobs(False))
        PRO_HI = len(PRO)

        def run(eng, job, before, after):
            n = 0
            for kind, arg in PRO:
                job(kind, arg, n, n + 1, None, 0, PRO[n - 1][0] if n else None)
                n += 1

            def entry(b, last):
                before(b)
                prev = "xT" if isinstance(b, int) and b == 0 else "y"
                hi = 0
                for i, (kind, arg) in enumerate(entry_jobs(last)):
                    hi += kind != "y"
                    job(kind, arg, len(PRO) + b * N + i, PRO_HI + b * N_HI + hi, b, i % 2, prev)
                    prev = kind
                after(b, len(PRO) + b * N + len(entry_jobs(last)))

            entry(0, False)
            with eng.Fori(1, B - 1) as b:
                entry(b, False)
            entry(B - 1, True)

        block = ctx.enter_context(nc.Block())

        @block.sync
        def _(sp):
            x_v = src.rearrange("b (t p) f -> b p t f", p=P)
            dst_v = dst.rearrange("b (t p) f -> b p t f", p=P)
            with nc.allow_non_contiguous_dma("a column per chunk"):
                sp.dma_start(b1c[:, :], b1.rearrange("(c p) -> p c", p=P)).then_inc(s_small, 16)
            sp.dma_start(b2b[:, :], b2.partition_broadcast(P)).then_inc(s_small, 16)
            sp.dma_start(ln_g[:, :], ln[0].partition_broadcast(P)).then_inc(s_small, 16)
            sp.dma_start(ln_b[:, :], ln[1].partition_broadcast(P)).then_inc(s_small, 16)
            for i in range(len(W_JOBS) // 2):
                if i >= 2:
                    sp.wait_ge(s_job, 2 * (i - 1))
                if i < FC // 2:
                    piece = w1[i * 2 * P:(i + 1) * 2 * P, :].rearrange("(t p) f -> p t f", p=P)
                else:
                    r, half = (i - FC // 2) // 2, i % 2
                    piece = w2[r * P:(r + 1) * P, half * 2 * D:(half + 1) * 2 * D].rearrange("p (t f) -> p t f", t=2)
                sp.dma_start(stage[i % 2][:, :, :], piece).then_inc(s_w[i % 2], 16)

            def load(b):
                sp.dma_start(x_raw[:, :, :], x_v[b]).then_inc(s_x, 16)

            def store(b):
                sp.wait_ge(s_fin, b + 1)
                sp.dma_start(dst_v[b], yo[:, :, :]).then_inc(s_store, 16)

            load(0)
            sp.wait_ge(s_yinit, 1)
            load(1)
            with sp.Fori(1, B - 1) as b:
                store(b - 1)
                sp.wait_ge(s_yinit, b + 1)
                load(b + 1)
            store(B - 2)
            store(B - 1)
            sp.wait_ge(s_store, 16 * B)

        @block.gpsimd
        def _(pool):
            make_identity(pool, ident, s_ident)

        @block.tensor
        def _(pe):
            def job(kind, arg, n, _, b, parity, prev):
                bank = job_ps[n % 2 if b is None else parity]
                if (kind, prev) in (("h", "xT"), ("y", "h")):
                    pe.wait_ge(s_job_done, n)
                elif b is not None or n >= 2:
                    pe.wait_ge(s_job_done, n - 1)
                if kind in ("w1T", "w2T"):
                    i = n // 2
                    if n % 2 == 0:
                        pe.wait_ge(s_w[i % 2], 16 * (i // 2 + 1))
                    tiles = [stage[i % 2][:, n % 2, c * P:(c + 1) * P] for c in range(KC)]
                elif kind == "xT":
                    nb = 0 if b is None else b + 1
                    pe.wait_ge(s_x, (nb + 1) * 16)
                    tiles = [x_raw[:, t, c * P:(c + 1) * P] for c in (2 * arg, 2 * arg + 1) for t in range(TB)]
                if kind in ("w1T", "w2T", "xT"):
                    for m, tile in enumerate(tiles):
                        mm = pe.transpose(bank[:, m * P:(m + 1) * P], tile, ident[:, :])
                elif kind == "h":
                    for c in range(2):
                        f = (2 * arg + c) * P
                        for kc in range(KC):
                            mm = matmul3(pe, bank[:, c * S:(c + 1) * S], [x[:, kc, f:f + P] for x in w1T],
                                         [x[:, kc, :] for x in xT], kc == 0, kc == KC - 1)
                else:
                    for fc in range(FC):
                        mm = matmul3(pe, bank[:, :], [x[:, fc, arg * P:(arg + 1) * P] for x in hT],
                                     [x[:, fc, :] for x in w2T], fc == 0, fc == FC - 1)
                mm.then_inc(s_job, 1)

            pe.wait_ge(s_ident, 2)
            run(pe, job, lambda b: None, lambda b, n: None)

        def transposed(part, kind, arg):
            if kind == "w1T":
                return w1T[part][:, :, arg * P:(arg + 1) * P]
            if kind == "w2T":
                r, g = arg
                return w2T[part][:, g * KC:(g + 1) * KC, r * P:(r + 1) * P]
            return xT[part][:, 2 * arg:2 * arg + 2, :]

        def bank_view(bank, kind):
            return bank[:, :].rearrange("p (c f) -> p c f", c=2 if kind == "xT" else KC)

        @block.scalar
        def _(act):
            def job(kind, arg, n, _, b, parity, prev):
                if kind == "y":
                    return
                bank = job_ps[n % 2 if b is None else parity]
                act.wait_ge(s_job, n + 1)
                if kind == "h":
                    for c in range(2):
                        m = 2 * arg + c
                        hi = act.activation(hidden[:, parity, c, :], bank[:, c * S:(c + 1) * S], ACT.Relu,
                                            bias=b1c[:, m:m + 1])
                else:
                    hi = act.activation(transposed(0, kind, arg), bank_view(bank, kind), ACT.Copy)
                hi.then_inc(s_job_hi, 1)

            act.wait_ge(s_small, 16 * 4)
            run(act, job, lambda b: None, lambda b, n: None)

        @block.vector
        def _(dve):
            def job(kind, arg, n, hi_jobs, b, parity, prev):
                bank = job_ps[n % 2 if b is None else parity]
                if kind == "y":
                    dve.wait_ge(s_job, n + 1)
                    lo = dve.tensor_tensor(y[:, arg, :], y[:, arg, :], bank[:, :], ALU.add)
                else:
                    dve.wait_ge(s_job_hi, hi_jobs)
                    if kind == "h":
                        sl = slice(2 * arg, 2 * arg + 2)
                        dve.tensor_copy(hT[0][:, sl, :], hidden[:, parity, :, :]).then_inc(s_split, 1)
                        dve.wait_ge(s_split, b * HJ + arg + 1)
                        lo = dve.tensor_tensor(hT[1][:, sl, :], hidden[:, parity, :, :], hT[0][:, sl, :],
                                               ALU.subtract)
                    else:
                        lo = dve.tensor_tensor(transposed(1, kind, arg), bank_view(bank, kind),
                                               transposed(0, kind, arg), ALU.subtract)
                lo.then_inc(s_job_done, 1)

            def residual(b):
                if not (isinstance(b, int) and b == 0):
                    dve.wait_ge(s_fin, b)
                dve.tensor_tensor(y[:, :, :], x_raw[:, :, :], b2b[:, :].unsqueeze(1).to_broadcast([P, TB, D]),
                                  ALU.add).then_inc(s_yinit, 1)
                dve.wait_ge(s_yinit, b + 1)

            def finish(b, jobs):
                if not (isinstance(b, int) and b == 0):
                    dve.wait_ge(s_store, 16 * b)
                dve.wait_ge(s_job_done, jobs)
                done = [0]

                def chain(ins):
                    done[0] += 1
                    ins.then_inc(s_ln, 1)
                    dve.wait_ge(s_ln, b * LN_CHAIN + done[0])
                layernorm_ops(dve, y, yo, stats, mv, ve, rs, ntmp, ln_g, ln_b, chain).then_inc(s_fin, 1)

            dve.wait_ge(s_small, 16 * 4)
            run(dve, job, residual, finish)


def xattn_decoder(nc, x, ctx_1024, mask_k, mask_qk, w, out):
    B = x.shape[0]

    def between(n):
        return nc.dram_tensor(f"x{n}", x.shape, F32, kind="Internal").ap()

    x1, x2, x3 = between(1), between(2), between(3)
    attention_phase(nc, "a0_", B, x, ctx_1024, [w[f"L0_xattn_w{n}"] for n in "qkvo"],
                    x1, 64, norm_w=w["L0_xattn_norm_w"])
    attention_phase(nc, "a1_", B, x1, None, [w[f"L1_xattn_sa_w{n}"] for n in "qkvo"], x2, 32,
                    bias=[w[f"L1_xattn_sa_b{n}"] for n in "qkvo"], mask=mask_qk,
                    ln=(w["L1_xattn_ln1_g"], w["L1_xattn_ln1_b"]))
    attention_phase(nc, "a2_", B, x2, ctx_1024, [w[f"L1_xattn_ca_w{n}"] for n in "qkvo"], x3, 32,
                    bias=[w[f"L1_xattn_ca_b{n}"] for n in "qkvo"], mask=mask_k,
                    ln=(w["L1_xattn_ln2_g"], w["L1_xattn_ln2_b"]))
    ffn_phase(nc, "f_", B, x3, w["L1_xattn_ffn_w1"], w["L1_xattn_ffn_b1"], w["L1_xattn_ffn_w2"],
              w["L1_xattn_ffn_b2"], (w["L1_xattn_ln3_g"], w["L1_xattn_ln3_b"]), out)


def kernel(**inputs):
    import numpy as np
    import concourse.bacc as bacc
    from concourse.bass_utils import run_bass_kernel_spmd

    nc = bacc.Bacc("TRN2", target_bir_lowering=False, num_devices=1)
    arrays, args = {}, {}
    for name, value in inputs.items():
        a = np.ascontiguousarray(value)
        arrays[f"in_{name}"] = a
        args[name] = nc.dram_tensor(f"in_{name}", a.shape, mybir.dt.from_np(a.dtype), kind="ExternalInput").ap()
    out = nc.dram_tensor("out", inputs["x"].shape, F32, kind="ExternalOutput").ap()
    xattn_decoder(nc, args["x"], args["ctx_1024"], args["mask_Bx1x1xS2_if1"], args["mask_Bx1xSxS2_if1"], args, out)
    return run_bass_kernel_spmd(nc, [arrays], core_ids=[0]).results[0]["out"]
```

```python
from contextlib import ExitStack

import concourse.bass as bass
from concourse import mybir

ALU = mybir.AluOpType
ACT = mybir.ActivationFunctionType
AX = mybir.AxisListType
F32 = mybir.dt.float32
F32R = mybir.dt.float32r
I32 = mybir.dt.int32

P = 128
D = 512
S = 256
H = 16
KC = D // P
TB = S // P
UF = 256
CU = UF // P
RMS_EPS = 1e-6
LN_EPS = 1e-5
MASKED = -1e30
RSQRT_SEED = float(0x5F3759DF)
RSQRT_STEPS = 3
RSQRT_OPS = 1 + 4 * RSQRT_STEPS

PARTS = ((0, 0), (0, 1), (1, 0))


def matmul3(pe, out, lhs, rhs, first, last):
    for n, (a, b) in enumerate(PARTS):
        mm = pe.matmul(out, lhs[a], rhs[b], start=first and n == 0, stop=last and n == 2)
    return mm


def rsqrt_ops(eng, v, r, t, chain):
    chain(eng.tensor_scalar(r.bitcast(I32), v.bitcast(I32), -0.5, RSQRT_SEED, ALU.mult, ALU.add))
    for _ in range(RSQRT_STEPS):
        chain(eng.tensor_tensor(t, v, r, ALU.mult))
        chain(eng.tensor_tensor(t, t, r, ALU.mult))
        chain(eng.tensor_scalar(t, t, -0.5, 1.5, ALU.mult, ALU.add))
        chain(eng.tensor_tensor(r, r, t, ALU.mult))


def make_identity(pool, ident, s_ident):
    pool.memset(ident[:, :], 0.0).then_inc(s_ident, 1)
    pool.wait_ge(s_ident, 1)
    pool.affine_select(out=ident[:, :], in_=ident[:, :], compare_op=ALU.not_equal, fill=1.0,
                       base=0, pattern=[[-1, P]], channel_multiplier=1).then_inc(s_ident, 1)


def chain_on(eng, s, base):
    done = [0]

    def chain(ins):
        done[0] += 1
        ins.then_inc(s, 1)
        eng.wait_ge(s, base + done[0])
        eng.nop(nofuse=True)
    return chain


def layernorm_stats(dve, y, stats, mv, s_bn, n, s_stats):
    for t in range(TB):
        last = dve.bn_stats(stats[:, t, :], y[:, t, :])
    last.then_inc(s_bn, 1)
    dve.wait_ge(s_bn, n + 1)
    dve.nop(nofuse=True)
    for t in range(TB):
        last = dve.bn_aggr(mv[:, t, :], stats[:, t, :])
    last.then_inc(s_stats, 1)


RMS_CHAIN = TB + RSQRT_OPS
LN_CHAIN = 1 + RSQRT_OPS + TB + 1


def layernorm_apply(pool, y, yo, mv, ve, rs, tmp, g, b, chain, s_y_free):
    chain(pool.tensor_scalar(ve[:, :], mv[:, :, 1], LN_EPS, None, ALU.add))
    rsqrt_ops(pool, ve[:, :], rs[:, :], tmp[:, :], chain)
    for t in range(TB):
        chain(pool.tensor_scalar(yo[:, t, :], y[:, t, :], mv[:, t, 0:1], rs[:, t:t + 1], ALU.subtract, ALU.mult))
    pool.sem_inc(s_y_free, 1)
    chain(pool.tensor_tensor(yo[:, :, :], yo[:, :, :], g[:, :].unsqueeze(1).to_broadcast([P, TB, D]), ALU.mult))
    return pool.tensor_tensor(yo[:, :, :], yo[:, :, :], b[:, :].unsqueeze(1).to_broadcast([P, TB, D]), ALU.add)


def attention_phase(nc, tag, B, src, kv, w, dst, d, norm_w=None, bias=None, mask=None, ln=None):
    DI = H * d
    U = DI // UF
    HU = UF // d
    assert U % 2 == 0 and B >= 3
    self_attention = kv is None
    transposed_weights = norm_w is None
    WQ, WK, WV, WO = (n * KC * DI for n in range(4))
    NW = 4 * KC * DI

    with ExitStack() as ctx:
        def sb(name, shape, dt):
            return ctx.enter_context(nc.sbuf_tensor(tag + name, shape, dt))

        def ps(name):
            return ctx.enter_context(nc.psum_tensor(tag + name, [P, 512], F32))

        def sem(name):
            return ctx.enter_context(nc.semaphore(tag + name))

        def pair(name, shape):
            return sb(name + "_hi", shape, F32R), sb(name + "_lo", shape, F32R)

        W = pair("w", [P, NW])
        xT = pair("xT", [P, KC, S])
        cT = xT if self_attention else pair("cT", [P, KC, S])
        q = pair("q", [P, 2, CU, S])
        k = pair("k", [P, 2, CU, S])
        v = pair("v", [P, 2, TB, (HU - 1) * P + d])
        pT = pair("pT", [P, 2, TB, S])
        oT = pair("oT", [P, CU, S])
        x_raw = sb("x_raw", [P, TB, D], F32)
        c_raw = sb("c_raw", [P, TB, D], F32)
        x_res = x_raw if HU == 4 else sb("x_res", [P, TB, D], F32)
        y = sb("y", [P, TB, D], F32)
        yo = sb("yo", [P, TB, D], F32)
        probs = sb("probs", [P, 2, TB, S], F32)
        ident = sb("ident", [P, P], F32)
        neg_max = sb("neg_max", [P, 2, TB], F32)
        row_sum = sb("row_sum", [P, 2, TB], F32)
        inv_sum = sb("inv_sum", [P, 2, TB], F32)
        if norm_w is not None:
            nw = sb("nw", [P, KC], F32)
            raw_max = sb("raw_max", [P, 2, TB], F32)
            squares = c_raw[:, 0, :]
            sumsq = sb("sumsq", [P, TB], F32)
            rstd_next = sb("rstd_next", [P, TB], F32)
            rstd = sb("rstd", [P, TB], F32)
            rtmp = sb("rtmp", [P, TB], F32)
        if mask is not None:
            mask_raw = sb("mask_raw", [P, TB, S], I32)
            mask_add = sb("mask_add", [P, TB, S], F32)
        if bias is not None:
            bqk = sb("bqk", [P, 2, KC], F32)
            bo = sb("bo", [P, D], F32)
            bv_raw = sb("bv_raw", [1, D], F32)
            bv = sb("bv_hi", [1, D], F32R), sb("bv_lo", [1, D], F32R)
            ones_f = sb("ones_f", [1, P], F32)
            ones = sb("ones", [1, P], F32R)
        if ln is not None:
            ln_g = sb("ln_g", [P, D], F32)
            ln_b = sb("ln_b", [P, D], F32)
            stats = sb("stats", [P, TB, 6], F32)
            mv = sb("mv", [P, TB, 2], F32)
            ve = sb("ve", [P, TB], F32)
            rs = sb("rs", [P, TB], F32)
            ntmp = sb("ntmp", [P, TB], F32)

        scores_ps = [ps("scores0"), ps("scores1")]
        probsT_ps = [ps("probsT0"), ps("probsT1")]
        out_ps = [ps("out0"), ps("out1")]
        job_ps = [ps("job0"), ps("job1")]

        s_x = sem("s_x")
        s_c = sem("s_c")
        s_m = sem("s_m")
        s_small = sem("s_small")
        NSTAGE = 3
        s_w = [sem(f"s_w{n}") for n in range(NSTAGE)]
        s_ident = sem("s_ident")
        s_whi = sem("s_whi")
        s_wlo = sem("s_wlo")
        s_bv = sem("s_bv")
        s_job = sem("s_job")
        s_job_hi = sem("s_job_hi")
        s_job_done = sem("s_job_done")
        s_scores = sem("s_scores")
        s_rawmax = sem("s_rawmax")
        s_max = sem("s_max")
        s_exp = sem("s_exp")
        s_probsT = sem("s_probsT")
        s_pT_hi = sem("s_pT_hi")
        s_pT_lo = sem("s_pT_lo")
        s_pv = sem("s_pv")
        s_zero = sem("s_zero")
        s_inv = sem("s_inv")
        s_norm = sem("s_norm")
        s_o_hi = sem("s_o_hi")
        s_o = sem("s_o")
        s_mask = sem("s_mask")
        s_rms = sem("s_rms")
        s_rstd = sem("s_rstd")
        s_x_free = sem("s_x_free")
        s_bn = sem("s_bn")
        s_stats = sem("s_stats")
        s_ln = sem("s_ln")
        s_y_free = sem("s_y_free")
        s_fin = sem("s_fin")
        s_store = sem("s_store")

        def pieces(u, step, prev2=True, nxt=True):
            un = (u + 1) % U
            new = u == U - 1

            def halves(kind):
                return [(kind, un, 0)] if nxt else [], [(kind, un, 1)] if nxt else []

            (q0, q1), (k0, k1), (v0, v1) = halves("q"), halves("k"), halves("v")
            wo0, wo1 = ([("wo", (t, (u - 2) % U), 1)] if prev2 else [] for t in range(TB))
            c, x = ([(kind, n, 1) for n in range(2)] if nxt and new else [] for kind in ("cT", "xT"))
            if self_attention:
                c = []
            if HU == 4:
                table = [(wo0 + c, wo1 + x), (q0, q1), (k0, k1), (v0, v1)]
            else:
                table = [(wo0, []), (c, wo1), (x, q0), (q1, []), ([], k0), (k1, []), (v0, []), (v1, [])]
            return table[step]

        def ending(part):
            return [(kind, arg) for kind, arg, half in part if half == 1]

        def jobs(u, step, **which):
            return [j for part in pieces(u, step, **which) for j in ending(part)]

        def load_jobs():
            return ([] if self_attention else [("cT", 0), ("cT", 1)]) + [("xT", 0), ("xT", 1)]

        def exist(seg, u):
            first, last = seg == "first", seg == "last"
            return dict(prev2=not (first and u < 2), nxt=not (last and u == U - 1))

        def seg_jobs(seg):
            return [j for u in range(U) for st in range(HU) for j in jobs(u, st, **exist(seg, u))]

        weight_jobs = [("wT", (n, r)) for n in range(4) for r in range(D // P)] if transposed_weights else []
        pro_jobs = weight_jobs + load_jobs() + [("q", 0), ("k", 0), ("v", 0)]
        FINISH = (1, 0) if HU == 4 else (1, 1)
        X_FREE = (2, 0) if HU == 4 else (0, 2)
        epi_jobs = [("wo", (0, U - 2)), ("wo", (1, U - 2)), ("wo", (0, U - 1)), ("wo", (1, U - 1))]

        def has_hi(kind):
            return kind != "wo"

        def counts(js):
            return len(js), sum(has_hi(kind) for kind, _ in js)

        N_PRO, N_FIRST, N_MID, N_LAST = (counts(x) for x in
                                         (pro_jobs, seg_jobs("first"), seg_jobs("mid"), seg_jobs("last")))
        assert N_MID[0] % 2 == 0

        class Place:

            def __init__(self, b, all_jobs, hi_jobs, parity, prev=None):
                self.b, self.base, self.hi_base, self.parity, self.prev = b, all_jobs, hi_jobs, parity, prev
                self.n = self.n_hi = self.slot_start = 0
                self.bank = None

            def next(self, kind):
                bank = job_ps[(self.parity + self.n) % 2]
                self.n += 1
                self.n_hi += has_hi(kind)
                self.prev = kind
                return bank

            @property
            def job(self):
                return self.base + self.n

            @property
            def hi_job(self):
                return self.hi_base + self.n_hi

        def run(eng, prologue, step, epilogue):
            def entry(seg, place):
                for u in range(U):
                    for st in range(HU):
                        step(place, seg, u, st)

            prologue(Place(None, 0, 0, 0))
            entry("first", Place(0, N_PRO[0], N_PRO[1], N_PRO[0]))
            b0 = tuple(N_PRO[n] + N_FIRST[n] for n in range(2))
            with eng.Fori(1, B - 1) as b:
                entry("mid", Place(b, (b - 1) * N_MID[0] + b0[0], (b - 1) * N_MID[1] + b0[1], b0[0]))
            b1 = tuple(b0[n] + (B - 2) * N_MID[n] for n in range(2))
            entry("last", Place(B - 1, b1[0], b1[1], b1[0]))
            e = tuple(b1[n] + N_LAST[n] for n in range(2))
            epilogue(Place(B, e[0], e[1], e[0], prev="v"))

        def head_wait(eng, s, seg, place, h, lag, count):
            if seg == "first" and h - lag + 1 <= 0:
                return
            eng.wait_ge(s, place.b * H + (h - lag + 1) if count is None else count)

        def unit_count(place, u):
            return place.b * U + (u + 1)

        def v_window(j):
            return j * P - j * d % P

        def v_columns(part, u):
            return v[part][:, u % 2, :, :].rearrange("p t (n e) -> p t n e", e=d)[:, :, ::P // d, :]

        def wT_out(part, n, r):
            return W[part][:, n * KC * D:(n + 1) * KC * D].rearrange("p (c f) -> p c f", c=KC)[:, :, r * P:(r + 1) * P]

        stage = [y[:, :, :], yo[:, :, :], probs[:, :, :, :].rearrange("p n t s -> p n (t s)")]

        PRO_PIECES = 4
        UNIT_PIECES = [("q", 0), ("k", 0), ("v", 0)] + [
            (kind, u + (kind != "wo")) for u in range(U) for kind in ("q", "k", "v", "wo")
            if kind == "wo" or u + 1 < U]
        PIECE_STAGE = [0, 1, 2] + [(0 if i % 2 and i < PRO_PIECES + 2 * HU else 1) for i in range(3, len(UNIT_PIECES))]

        def pieces_in_step(u, j):
            i = PRO_PIECES + u * HU + j
            return [i] if not transposed_weights and i < len(UNIT_PIECES) else []

        def piece_load(i):
            return 16 * PIECE_STAGE[:i + 1].count(PIECE_STAGE[i])

        def piece_view(part, i):
            kind, u = UNIT_PIECES[i]
            if kind == "wo":
                return W[part][:, WO + u * CU * D:WO + (u + 1) * CU * D].rearrange("p (c f) -> p c f", c=CU)
            off = {"q": WQ, "k": WK, "v": WV}[kind]
            return W[part][:, off:off + KC * DI].rearrange("p (c f) -> p c f", c=KC)[:, :, u * UF:(u + 1) * UF]

        def piece_raw(i):
            raw = stage[PIECE_STAGE[i]].rearrange("p t f -> p (t f)")
            return raw.rearrange("p (c f) -> p c f", c=CU if UNIT_PIECES[i][0] == "wo" else KC)

        block = ctx.enter_context(nc.Block())

        @block.sync
        def _(sp):
            x_v = src.rearrange("b (t p) f -> b p t f", p=P)
            dst_v = dst.rearrange("b (t p) f -> b p t f", p=P)

            def load_x(b):
                sp.dma_start(x_raw[:, :, :], x_v[b]).then_inc(s_x, 16)
                if mask is not None:
                    if mask.shape[2] == 1:
                        sp.dma_start(mask_raw[:, 0, :], mask[b, 0, 0].partition_broadcast(P)).then_inc(s_m, 16)
                        sp.dma_start(mask_raw[:, 1, :], mask[b, 0, 0].partition_broadcast(P)).then_inc(s_m, 16)
                    else:
                        m_v = mask.rearrange("b a (t p) k -> (b a) p t k", p=P)
                        sp.dma_start(mask_raw[:, :, :], m_v[b]).then_inc(s_m, 16)

            def load_c(b):
                if not self_attention:
                    sp.dma_start(c_raw[:, :, :], kv.rearrange("b (t p) f -> b p t f", p=P)[b]).then_inc(s_c, 16)

            def store(b):
                sp.wait_ge(s_fin, b + 1)
                sp.nop(nofuse=True)
                sp.dma_start(dst_v[b], yo[:, :, :]).then_inc(s_store, 16)

            AHEAD = 2

            def load_piece(i):
                if PIECE_STAGE[i] in PIECE_STAGE[:i]:
                    before = max(n for n in range(i) if PIECE_STAGE[n] == PIECE_STAGE[i])
                    sp.wait_ge(s_wlo, before + 1)
                kind, u = UNIT_PIECES[i]
                if kind == "wo":
                    piece = w[3][u * UF:(u + 1) * UF, :].rearrange("(c p) f -> p c f", p=P)
                else:
                    n = ("q", "k", "v").index(kind)
                    piece = w[n][:, u * UF:(u + 1) * UF].rearrange("(c p) f -> p c f", p=P)
                sp.dma_start(piece_raw(i), piece).then_inc(s_w[PIECE_STAGE[i]], 16)

            if not transposed_weights:
                load_c(0)
                load_x(0)
            if norm_w is not None:
                with nc.allow_non_contiguous_dma("a column per chunk"):
                    sp.dma_start(nw[:, :], norm_w.rearrange("(c p) -> p c", p=P)).then_inc(s_small, 16)
            if transposed_weights:
                for i in range(4 * D // (TB * P)):
                    if i == NSTAGE:
                        load_c(0)
                        load_x(0)
                    if i >= NSTAGE:
                        sp.wait_ge(s_job, TB * (i - NSTAGE + 1))
                    n, half = i // 2, i % 2
                    sp.dma_start(stage[i % NSTAGE], w[n][half * S:(half + 1) * S, :].rearrange(
                        "(t p) f -> p t f", p=P)).then_inc(s_w[i % NSTAGE], 16)
            else:
                for i in range(PRO_PIECES + AHEAD):
                    load_piece(i)
            if bias is not None:
                with nc.allow_non_contiguous_dma("a column per chunk"):
                    sp.dma_start(bqk[:, 0, :], bias[0].rearrange("(c p) -> p c", p=P)).then_inc(s_small, 16)
                    sp.dma_start(bqk[:, 1, :], bias[1].rearrange("(c p) -> p c", p=P)).then_inc(s_small, 16)
                sp.dma_start(bv_raw[:, :], bias[2].rearrange("(a f) -> a f", a=1)).then_inc(s_small, 16)
                sp.dma_start(bo[:, :], bias[3].partition_broadcast(P)).then_inc(s_small, 16)
                sp.dma_start(ln_g[:, :], ln[0].partition_broadcast(P)).then_inc(s_small, 16)
                sp.dma_start(ln_b[:, :], ln[1].partition_broadcast(P)).then_inc(s_small, 16)

            def prologue(place):
                for kind, _ in pro_jobs:
                    place.next(kind)

            def step(place, seg, u, j):
                if u == 0 and j == 0 and seg != "last" and not self_attention:
                    sp.wait_ge(s_job, place.job)
                    if norm_w is not None:
                        sp.wait_ge(s_rms, (place.b + 1) * RMS_CHAIN)
                    sp.nop(nofuse=True)
                    load_c(place.b + 1)
                for kind, _ in jobs(u, j, **exist(seg, u)):
                    place.next(kind)
                if seg == "first":
                    for i in pieces_in_step(u, j):
                        if i + AHEAD < len(UNIT_PIECES):
                            load_piece(i + AHEAD)
                if (u, j) == X_FREE and seg != "last":
                    if x_res is x_raw:
                        sp.wait_ge(s_job_done, place.job)
                    else:
                        sp.wait_ge(s_x_free, place.b + 1)
                    sp.nop(nofuse=True)
                    load_x(place.b + 1)
                if (u, j) == FINISH and seg != "first":
                    store(place.b - 1)

            def epilogue(place):
                store(B - 1)
                sp.wait_ge(s_store, 16 * B)

            run(sp, prologue, step, epilogue)

        @block.gpsimd
        def _(pool):
            make_identity(pool, ident, s_ident)
            for part in v:
                pool.memset(part[:, :, :, :].bitcast(F32), 0.0).then_inc(s_zero, 1)

            def finish(place, b):
                if ln is None:
                    pool.wait_ge(s_job_done, place.job)
                else:
                    pool.wait_ge(s_stats, b + 1)
                if not (isinstance(b, int) and b == 0):
                    pool.wait_ge(s_store, 16 * b)
                pool.nop(nofuse=True)
                if ln is None:
                    pool.tensor_copy(yo[:, :, :], y[:, :, :]).then_inc(s_fin, 1)
                else:
                    layernorm_apply(pool, y, yo, mv, ve, rs, ntmp, ln_g, ln_b,
                                    chain_on(pool, s_ln, b * LN_CHAIN), s_y_free).then_inc(s_fin, 1)

            def prologue(place):
                for kind, _ in pro_jobs:
                    place.next(kind)

            def step(place, seg, u, j):
                for kind, _ in jobs(u, j, **exist(seg, u)):
                    place.next(kind)
                if (u, j) == FINISH and seg != "first":
                    finish(place, place.b - 1)

            def epilogue(place):
                for kind, _ in epi_jobs:
                    place.next(kind)
                finish(place, B - 1)

            if bias is not None:
                pool.wait_ge(s_small, 16 * 6)
                pool.sem_inc(s_y_free, 1)
            run(pool, prologue, step, epilogue)

        @block.tensor
        def _(pe):
            def transposes(bank, tiles):
                for n, t in enumerate(tiles):
                    tr = pe.transpose(bank[:, n * P:(n + 1) * P], t, ident[:, :])
                return tr

            def piece(place, kind, arg, half):
                if kind in ("q", "k", "v"):
                    first, last = half == 0, half == 1
                else:
                    first = last = True
                if first:
                    start_job(place, kind)
                mm = run_job(place, place.bank, kind, arg, (half,) if kind in ("q", "k", "v") else (0, 1))
                if last:
                    mm.then_inc(s_job, 1)

            def job(place, kind, arg):
                start_job(place, kind)
                run_job(place, place.bank, kind, arg, (0, 1)).then_inc(s_job, 1)

            def start_job(place, kind):
                n, prev = place.job, place.prev
                place.bank = place.next(kind)
                if (kind, prev) in (("q", "xT"), ("k", "cT")):
                    pe.wait_ge(s_job_done, n)
                elif place.b is not None or n >= 2:
                    pe.wait_ge(s_job_done, n - 1)

            def run_job(place, bank, kind, arg, halves):
                if kind == "wT":
                    wi, r = arg
                    i = wi * 2 + r // 2
                    if r % 2 == 0:
                        pe.wait_ge(s_w[i % NSTAGE], 16 * (i // NSTAGE + 1))
                    mm = transposes(bank, [stage[i % NSTAGE][:, r % 2, c * P:(c + 1) * P] for c in range(KC)])
                elif kind in ("xT", "cT"):
                    raw = x_raw if kind == "xT" else c_raw
                    nb = 0 if place.b is None else place.b + 1
                    pe.wait_ge(s_x if kind == "xT" else s_c, (nb + 1) * 16)
                    mm = transposes(bank, [raw[:, t, c * P:(c + 1) * P] for c in (2 * arg, 2 * arg + 1)
                                           for t in range(TB)])
                elif kind in ("q", "k"):
                    a = xT if kind == "q" else cT
                    off = WQ if kind == "q" else WK
                    weight_wait(place, kind, arg)
                    for c in halves:
                        for kc in range(KC):
                            f = off + kc * DI + arg * UF + c * P
                            mm = matmul3(pe, bank[:, c * S:(c + 1) * S], [x[:, f:f + P] for x in W],
                                         [x[:, kc, :] for x in a], kc == 0, kc == KC - 1)
                elif kind == "v":
                    weight_wait(place, kind, arg)
                    for t in halves:
                        out = bank[:, t * UF:(t + 1) * UF]
                        for kc in range(KC):
                            f = WV + kc * DI + arg * UF
                            mm = matmul3(pe, out, [x[:, kc, t * P:(t + 1) * P] for x in cT],
                                         [x[:, f:f + UF] for x in W], kc == 0, kc == KC - 1 and bias is None)
                        if bias is not None:
                            pe.matmul(out, ones[:, :], bv[0][:, arg * UF:(arg + 1) * UF], start=False, stop=False)
                            mm = pe.matmul(out, ones[:, :], bv[1][:, arg * UF:(arg + 1) * UF], start=False, stop=True)
                else:
                    t, u = arg
                    weight_wait(place, kind, u)
                    if t == 0:
                        pe.wait_ge(s_o, unit_count(place, u - U if u >= U - 2 else u))
                    for c in range(CU):
                        f = WO + (u * CU + c) * D
                        mm = matmul3(pe, bank[:, :], [x[:, c, t * P:(t + 1) * P] for x in oT],
                                     [x[:, f:f + D] for x in W], c == 0, c == CU - 1)
                return mm

            def weight_wait(place, kind, u):
                first_use = place.b is None or isinstance(place.b, int) and place.b == 0 or kind == "wo" and u >= U - 2
                if not transposed_weights and first_use:
                    pe.wait_ge(s_wlo, UNIT_PIECES.index((kind, u)) + 1)

            def scores(place, seg, u, j):
                h = u * HU + j
                if j == 0:
                    pe.wait_ge(s_job_done, place.job - 1)
                head_wait(pe, s_exp, seg, place, h, 2, None)
                bank = scores_ps[h % 2]
                c, r = j * d // P, j * d % P
                for t in range(TB):
                    mm = matmul3(pe, bank[:, t * S:(t + 1) * S],
                                 [x[r:r + d, u % 2, c, t * P:(t + 1) * P] for x in q],
                                 [x[r:r + d, u % 2, c, :] for x in k], True, True)
                mm.then_inc(s_scores, 1)

            def transpose_probs(place, seg, h):
                head_wait(pe, s_norm, seg, place, h, 0, None)
                head_wait(pe, s_pT_lo, seg, place, h, 2, None)
                hb = h % 2
                transposes(probsT_ps[hb], [probs[:, hb, t, kb * P:(kb + 1) * P] for kb in range(TB)
                                           for t in range(TB)]).then_inc(s_probsT, 1)

            def attend(place, seg, h, v_jobs):
                j, ub = h % HU, (h // HU) % 2
                if j == 0:
                    pe.wait_ge(s_job_done, v_jobs)
                    if not (seg == "first" and h < 2 * HU):
                        pe.wait_ge(s_o, unit_count(place, h // HU) - 2)
                head_wait(pe, s_pT_lo, seg, place, h, 0, None)
                c, r = j * d // P, j * d % P
                for kb in range(TB):
                    mm = matmul3(pe, out_ps[ub][:, c * S:(c + 1) * S],
                                 [x[:, ub, kb, v_window(j):v_window(j) + P] for x in v],
                                 [x[:, h % 2, kb, :] for x in pT],
                                 r == 0 and kb == 0, r == P - d and kb == TB - 1)
                mm.then_inc(s_pv, 1)

            def prologue(place):
                pe.wait_ge(s_ident, 2)
                for kind, arg in pro_jobs:
                    if bias is not None and kind == "v":
                        pe.wait_ge(s_bv, 4)
                    job(place, kind, arg)

            def step(place, seg, u, j):
                h = u * HU + j
                if j == 0:
                    place.slot_start = place.job
                early, late = pieces(u, j, **exist(seg, u))
                scores(place, seg, u, j)
                if h >= 2 or seg != "first":
                    transpose_probs(place, seg, h - 2)
                for kind, arg, half in early:
                    piece(place, kind, arg, half)
                if h >= 3 or seg != "first":
                    attend(place, seg, h - 3, place.slot_start)
                for kind, arg, half in late:
                    piece(place, kind, arg, half)

            def epilogue(place):
                transpose_probs(place, "epi", -2)
                attend(place, "epi", -3, None)
                transpose_probs(place, "epi", -1)
                attend(place, "epi", -2, None)
                attend(place, "epi", -1, None)
                for kind, arg in epi_jobs:
                    job(place, kind, arg)

            run(pe, prologue, step, epilogue)

        @block.scalar
        def _(act):
            def job(place, kind, arg):
                bank = place.next(kind)
                if not has_hi(kind):
                    return
                act.wait_ge(s_job, place.job)
                if kind == "wT":
                    hi = act.activation(wT_out(0, *arg), bank[:, :].rearrange("p (c f) -> p c f", c=KC), ACT.Copy)
                elif kind in ("xT", "cT"):
                    a = xT if kind == "xT" else cT
                    hi = act.activation(a[0][:, 2 * arg:2 * arg + 2, :],
                                        bank[:, :].rearrange("p (c t) -> p c t", c=2), ACT.Copy)
                elif kind in ("q", "k"):
                    out = (q if kind == "q" else k)[0][:, arg % 2, :, :]
                    if bias is None:
                        hi = act.activation(out, bank[:, :].rearrange("p (c t) -> p c t", c=CU), ACT.Copy)
                    else:
                        for c in range(CU):
                            b_col = bqk[:, int(kind == "k"), arg * CU + c:arg * CU + c + 1]
                            hi = act.activation(out[:, c, :], bank[:, c * S:(c + 1) * S], ACT.Identity, bias=b_col)
                else:
                    if place.b is None:
                        act.wait_ge(s_zero, 2)
                    hi = act.activation(v_columns(0, arg), bank[:, :].rearrange("p (t h e) -> p t h e", t=TB, h=HU),
                                        ACT.Copy)
                hi.then_inc(s_job_hi, 1)

            def weights_hi(i):
                act.wait_ge(s_w[PIECE_STAGE[i]], piece_load(i))
                out, raw = piece_view(0, i), piece_raw(i)
                if UNIT_PIECES[i][0] == "q":
                    for c in range(KC):
                        hi = act.activation(out[:, c, :], raw[:, c, :], ACT.Copy, scale=nw[:, c:c + 1])
                else:
                    hi = act.activation(out, raw, ACT.Copy)
                hi.then_inc(s_whi, 1)

            def exps(place, seg, u, j):
                h = u * HU + j
                head_wait(act, s_max, seg, place, h, 0, None)
                head_wait(act, s_probsT, seg, place, h, 2, None)
                for t in range(TB):
                    scale = rstd[:, t:t + 1] if norm_w is not None else -1.0
                    e = act.activation(probs[:, h % 2, t, :], scores_ps[h % 2][:, t * S:(t + 1) * S], ACT.Exp,
                                       bias=neg_max[:, h % 2, t:t + 1], scale=scale,
                                       accum_out=row_sum[:, h % 2, t:t + 1])
                e.then_inc(s_exp, 1)

            def normalise(place, seg, h):
                head_wait(act, s_inv, seg, place, h, 0, None)
                for t in range(TB):
                    n = act.activation(probs[:, h % 2, t, :], probs[:, h % 2, t, :], ACT.Copy,
                                       scale=inv_sum[:, h % 2, t:t + 1])
                n.then_inc(s_norm, 1)

            def unit_output(place, u):
                n = unit_count(place, u)
                act.wait_ge(s_pv, n * HU)
                act.wait_ge(s_job, place.job)
                act.activation(oT[0][:, :, :], out_ps[u % 2][:, :].rearrange("p (c t) -> p c t", c=CU),
                               ACT.Copy).then_inc(s_o_hi, 1)

            def probsT_hi(place, seg, h):
                head_wait(act, s_probsT, seg, place, h, 0, None)
                head_wait(act, s_pv, seg, place, h, 2, None)
                act.activation(pT[0][:, h % 2, :, :], probsT_ps[h % 2][:, :].rearrange("p (k t) -> p k t", k=TB),
                               ACT.Copy).then_inc(s_pT_hi, 1)

            def prologue(place):
                if not transposed_weights:
                    act.wait_ge(s_small, 16)
                for kind, arg in pro_jobs:
                    if not transposed_weights and (kind, arg) in UNIT_PIECES:
                        weights_hi(UNIT_PIECES.index((kind, arg)))
                    if bias is not None and (kind, arg) == ("q", 0):
                        act.wait_ge(s_bv, 1)
                        act.wait_ge(s_small, 16 * 6)
                        act.activation(ones[:, :], ones_f[:, :], ACT.Copy).then_inc(s_bv, 1)
                        act.activation(bv[0][:, :], bv_raw[:, :], ACT.Copy).then_inc(s_bv, 1)
                    job(place, kind, arg)
                if not transposed_weights:
                    for i in range(3, PRO_PIECES):
                        weights_hi(i)

            def step(place, seg, u, j):
                h = u * HU + j
                early, late = pieces(u, j, **exist(seg, u))
                if j == 3 and (u >= 1 or seg != "first"):
                    unit_output(place, u - 1)
                if h >= 2 or seg != "first":
                    probsT_hi(place, seg, h - 2)
                exps(place, seg, u, j)
                normalise(place, seg, h)
                if seg == "first":
                    for i in pieces_in_step(u, j):
                        weights_hi(i)
                for kind, arg in ending(early):
                    job(place, kind, arg)
                for kind, arg in ending(late):
                    job(place, kind, arg)

            def epilogue(place):
                probsT_hi(place, "epi", -2)
                probsT_hi(place, "epi", -1)
                for kind, arg in epi_jobs:
                    if (kind, arg) == ("wo", (0, U - 1)):
                        unit_output(place, -1)
                    job(place, kind, arg)

            run(act, prologue, step, epilogue)

        @block.vector
        def _(dve):
            def job(place, kind, arg):
                n = place.job
                bank = place.next(kind)
                if has_hi(kind):
                    dve.wait_ge(s_job_hi, place.hi_job)
                if kind == "wT":
                    lo = dve.tensor_tensor(wT_out(1, *arg), bank[:, :].rearrange("p (c f) -> p c f", c=KC),
                                           wT_out(0, *arg), ALU.subtract)
                elif kind in ("xT", "cT"):
                    a = xT if kind == "xT" else cT
                    sl = slice(2 * arg, 2 * arg + 2)
                    lo = dve.tensor_tensor(a[1][:, sl, :], bank[:, :].rearrange("p (c t) -> p c t", c=2),
                                           a[0][:, sl, :], ALU.subtract)
                elif kind in ("q", "k"):
                    a = q if kind == "q" else k
                    hi, out = a[0][:, arg % 2, :, :], a[1][:, arg % 2, :, :]
                    if bias is None:
                        lo = dve.tensor_tensor(out, bank[:, :].rearrange("p (c t) -> p c t", c=CU), hi, ALU.subtract)
                    else:
                        for c in range(CU):
                            b_col = bqk[:, int(kind == "k"), arg * CU + c:arg * CU + c + 1]
                            lo = dve.scalar_tensor_tensor(out=out[:, c, :], in0=bank[:, c * S:(c + 1) * S],
                                                          scalar=b_col, in1=hi[:, c, :], op0=ALU.add,
                                                          op1=ALU.subtract)
                elif kind == "v":
                    lo = dve.tensor_tensor(v_columns(1, arg), bank[:, :].rearrange("p (t h e) -> p t h e", t=TB, h=HU),
                                           v_columns(0, arg), ALU.subtract)
                else:
                    t, unit = arg
                    if unit == 0 and t == 0:
                        b = place.b if HU == 4 else place.b - 1
                        if not (isinstance(b, int) and b == 0):
                            if ln is None:
                                dve.wait_ge(s_fin, b)
                            else:
                                dve.wait_ge(s_y_free, b + 1)
                    dve.wait_ge(s_job, place.job)
                    dve.wait_ge(s_job_done, n)
                    lo = dve.tensor_tensor(y[:, t, :], (x_res if unit == 0 else y)[:, t, :], bank[:, :], ALU.add)
                lo.then_inc(s_job_done, 1)

            def rstd_of_next(nb):
                chain = chain_on(dve, s_rms, nb * RMS_CHAIN)
                dve.wait_ge(s_x, (nb + 1) * 16)
                for t in range(TB):
                    chain(dve.tensor_tensor_reduce(out=squares, in0=x_raw[:, t, :], in1=x_raw[:, t, :],
                                                   scale=1.0 / D, scalar=RMS_EPS, op0=ALU.mult, op1=ALU.add,
                                                   accum_out=sumsq[:, t:t + 1]))
                rsqrt_ops(dve, sumsq[:, :], rstd_next[:, :], rtmp[:, :], chain)

            def weights_lo(i):
                dve.wait_ge(s_w[PIECE_STAGE[i]], piece_load(i))
                dve.wait_ge(s_whi, i + 1)
                hi, out, raw = piece_view(0, i), piece_view(1, i), piece_raw(i)
                if UNIT_PIECES[i][0] == "q":
                    for c in range(KC):
                        lo = dve.scalar_tensor_tensor(out=out[:, c, :], in0=raw[:, c, :], scalar=nw[:, c:c + 1],
                                                      in1=hi[:, c, :], op0=ALU.mult, op1=ALU.subtract)
                else:
                    lo = dve.tensor_tensor(out, raw, hi, ALU.subtract)
                lo.then_inc(s_wlo, 1)

            def maxima(place, seg, u, j):
                h = u * HU + j
                hb = h % 2
                if h == 0:
                    if norm_w is not None:
                        if seg != "first":
                            dve.wait_ge(s_exp, place.b * H)
                        dve.tensor_copy(rstd[:, :], rstd_next[:, :]).then_inc(s_rstd, 1)
                        dve.wait_ge(s_rstd, place.b + 1)
                    if mask is not None:
                        if seg != "first":
                            dve.wait_ge(s_max, place.b * H)
                        dve.wait_ge(s_m, (place.b + 1) * (32 if mask.shape[2] == 1 else 16))
                        dve.tensor_scalar(mask_add[:, :, :], mask_raw[:, :, :], 0.0, MASKED, ALU.is_equal,
                                          ALU.mult).then_inc(s_mask, 1)
                        dve.wait_ge(s_mask, place.b + 1)
                head_wait(dve, s_scores, seg, place, h, 0, None)
                bank = scores_ps[hb]
                if norm_w is not None:
                    dve.tensor_reduce(raw_max[:, hb, :], bank[:, :].rearrange("p (t k) -> p t k", t=TB), AX.X,
                                      ALU.max, negate=True).then_inc(s_rawmax, 1)
                    head_wait(dve, s_rawmax, seg, place, h, 0, None)
                    dve.tensor_tensor(neg_max[:, hb, :], raw_max[:, hb, :], rstd[:, :],
                                      ALU.mult).then_inc(s_max, 1)
                else:
                    dve.nop(nofuse=True)
                    for t in range(TB):
                        m = dve.tensor_tensor_reduce(out=bank[:, t * S:(t + 1) * S], in0=bank[:, t * S:(t + 1) * S],
                                                     in1=mask_add[:, t, :], scale=-float(d) ** -0.5, scalar=3e38,
                                                     op0=ALU.add, op1=ALU.min, accum_out=neg_max[:, hb, t:t + 1])
                    m.then_inc(s_max, 1)

            def probsT_lo(place, seg, h):
                head_wait(dve, s_pT_hi, seg, place, h, 0, None)
                hb = h % 2
                dve.tensor_tensor(pT[1][:, hb, :, :], probsT_ps[hb][:, :].rearrange("p (k t) -> p k t", k=TB),
                                  pT[0][:, hb, :, :], ALU.subtract).then_inc(s_pT_lo, 1)

            def inverse(place, seg, h):
                head_wait(dve, s_exp, seg, place, h, 0, None)
                dve.reciprocal(inv_sum[:, h % 2, :], row_sum[:, h % 2, :]).then_inc(s_inv, 1)

            def unit_output(place, u):
                dve.wait_ge(s_o_hi, unit_count(place, u))
                dve.tensor_tensor(oT[1][:, :, :], out_ps[u % 2][:, :].rearrange("p (c t) -> p c t", c=CU),
                                  oT[0][:, :, :], ALU.subtract).then_inc(s_o, 1)

            def statistics(place, b):
                dve.wait_ge(s_job_done, place.job)
                if not (isinstance(b, int) and b == 0):
                    dve.wait_ge(s_ln, b * LN_CHAIN)
                layernorm_stats(dve, y, stats, mv, s_bn, b, s_stats)

            def residual(place):
                if x_res is x_raw:
                    return
                dve.tensor_tensor(x_res[:, :, :], x_raw[:, :, :], bo[:, :].unsqueeze(1).to_broadcast([P, TB, D]),
                                  ALU.add).then_inc(s_x_free, 1)
                dve.wait_ge(s_x_free, place.b + 1)

            def prologue(place):
                if not transposed_weights:
                    dve.wait_ge(s_small, 16)
                for kind, arg in pro_jobs:
                    if norm_w is not None and (kind, arg) == ("q", 0):
                        rstd_of_next(0)
                    if not transposed_weights and (kind, arg) in UNIT_PIECES:
                        weights_lo(UNIT_PIECES.index((kind, arg)))
                    if bias is not None and (kind, arg) == ("q", 0):
                        dve.memset(ones_f[:, :], 1.0).then_inc(s_bv, 1)
                        dve.wait_ge(s_bv, 3)
                        dve.wait_ge(s_small, 16 * 6)
                        dve.tensor_tensor(bv[1][:, :], bv_raw[:, :], bv[0][:, :], ALU.subtract).then_inc(s_bv, 1)
                    job(place, kind, arg)
                if not transposed_weights:
                    for i in range(3, PRO_PIECES):
                        weights_lo(i)

            def step(place, seg, u, j):
                h = u * HU + j
                early, late = pieces(u, j, **exist(seg, u))
                if j == 3 and (u >= 1 or seg != "first"):
                    unit_output(place, u - 1)
                maxima(place, seg, u, j)
                if h >= 2 or seg != "first":
                    probsT_lo(place, seg, h - 2)
                inverse(place, seg, h)
                if seg == "first":
                    for i in pieces_in_step(u, j):
                        weights_lo(i)
                for kind, arg in ending(early):
                    job(place, kind, arg)
                for kind, arg in ending(late):
                    job(place, kind, arg)
                if (u, j) == FINISH and seg != "first" and ln is not None:
                    statistics(place, place.b - 1)
                if (u, j) == X_FREE:
                    residual(place)
                if norm_w is not None and u == U - 1 and j == HU - 1 and seg != "last":
                    rstd_of_next(place.b + 1)

            def epilogue(place):
                probsT_lo(place, "epi", -2)
                probsT_lo(place, "epi", -1)
                for kind, arg in epi_jobs:
                    if (kind, arg) == ("wo", (0, U - 1)):
                        unit_output(place, -1)
                    job(place, kind, arg)
                if ln is not None:
                    statistics(place, B - 1)

            run(dve, prologue, step, epilogue)


def ffn_phase(nc, tag, B, src, w1, b1, w2, b2, ln, dst):
    F = w1.shape[0]
    FC = F // P
    HJ = FC // 2
    W1N, W2N = KC * F, FC * D
    assert B >= 3

    with ExitStack() as ctx:
        def sb(name, shape, dt):
            return ctx.enter_context(nc.sbuf_tensor(tag + name, shape, dt))

        def sem(name):
            return ctx.enter_context(nc.semaphore(tag + name))

        def pair(name, shape):
            return sb(name + "_hi", shape, F32R), sb(name + "_lo", shape, F32R)

        w1T = pair("w1T", [P, KC, F])
        w2T = pair("w2T", [P, FC, D])
        xT = pair("xT", [P, KC, S])
        hT = pair("hT", [P, FC, S])
        hidden = sb("hidden", [P, 4, 2, S], F32)
        x_raw = sb("x_raw", [P, TB, D], F32)
        y = sb("y", [P, TB, D], F32)
        yo = sb("yo", [P, TB, D], F32)
        ident = sb("ident", [P, P], F32)
        b1c = sb("b1c", [P, FC], F32)
        b2b = sb("b2b", [P, D], F32)
        ln_g = sb("ln_g", [P, D], F32)
        ln_b = sb("ln_b", [P, D], F32)
        stats = sb("stats", [P, TB, 6], F32)
        mv = sb("mv", [P, TB, 2], F32)
        ve = sb("ve", [P, TB], F32)
        rs = sb("rs", [P, TB], F32)
        ntmp = sb("ntmp", [P, TB], F32)
        NB = 4
        job_ps = [ctx.enter_context(nc.psum_tensor(f"{tag}job{n}", [P, 512], F32)) for n in range(NB)]

        s_ident = sem("s_ident")
        s_small = sem("s_small")
        s_w = [sem(f"s_w{n}") for n in range(4)]
        s_x = sem("s_x")
        s_job = sem("s_job")
        s_job_hi = sem("s_job_hi")
        s_job_done = sem("s_job_done")
        s_split = sem("s_split")
        s_yinit = sem("s_yinit")
        s_bn = sem("s_bn")
        s_stats = sem("s_stats")
        s_ln = sem("s_ln")
        s_y_free = sem("s_y_free")
        s_fin = sem("s_fin")
        s_store = sem("s_store")

        stage = [y, yo, hidden[:, 0:2].rearrange("p t n s -> p t (n s)"),
                 hidden[:, 2:4].rearrange("p t n s -> p t (n s)")]
        NSTAGE = len(stage)
        W_JOBS = [("w1T", r) for r in range(FC)] + [("w2T", (r, g)) for r in range(D // P) for g in range(KC)]
        PRO = W_JOBS + [("xT", 0), ("xT", 1)]

        def entry_jobs(last):
            return [("h", n) for n in range(HJ)] + ([] if last else [("xT", 0), ("xT", 1)]) + [("y", 0), ("y", 1)]

        N = len(entry_jobs(False))
        assert N % NB == 0

        N_HI = sum(kind != "y" for kind, _ in entry_jobs(False))
        PRO_HI = len(PRO)

        def run(eng, job, after):
            n = 0
            for kind, arg in PRO:
                job(kind, arg, n, n + 1, None, n % NB, PRO[n - 1][0] if n else None)
                n += 1

            def entry(b, last):
                prev = "xT" if isinstance(b, int) and b == 0 else "y"
                hi = 0
                for i, (kind, arg) in enumerate(entry_jobs(last)):
                    hi += kind != "y"
                    job(kind, arg, len(PRO) + b * N + i, PRO_HI + b * N_HI + hi, b,
                        (len(PRO) + i) % NB, prev)
                    prev = kind
                after(b, len(PRO) + b * N + len(entry_jobs(last)))

            entry(0, False)
            with eng.Fori(1, B - 1) as b:
                entry(b, False)
            entry(B - 1, True)

        block = ctx.enter_context(nc.Block())

        @block.sync
        def _(sp):
            x_v = src.rearrange("b (t p) f -> b p t f", p=P)
            dst_v = dst.rearrange("b (t p) f -> b p t f", p=P)
            for i in range(len(W_JOBS) // 2):
                if i >= NSTAGE:
                    sp.wait_ge(s_job, 2 * (i - NSTAGE + 1))
                if i < FC // 2:
                    piece = w1[i * 2 * P:(i + 1) * 2 * P, :].rearrange("(t p) f -> p t f", p=P)
                else:
                    r, half = (i - FC // 2) // 2, i % 2
                    piece = w2[r * P:(r + 1) * P, half * 2 * D:(half + 1) * 2 * D].rearrange("p (t f) -> p t f", t=2)
                sp.dma_start(stage[i % NSTAGE][:, :, :], piece).then_inc(s_w[i % NSTAGE], 16)

            def load(b):
                sp.dma_start(x_raw[:, :, :], x_v[b]).then_inc(s_x, 16)

            def store(b):
                sp.wait_ge(s_fin, b + 1)
                sp.dma_start(dst_v[b], yo[:, :, :]).then_inc(s_store, 16)

            load(0)
            with nc.allow_non_contiguous_dma("a column per chunk"):
                sp.dma_start(b1c[:, :], b1.rearrange("(c p) -> p c", p=P)).then_inc(s_small, 16)
            sp.dma_start(b2b[:, :], b2.partition_broadcast(P)).then_inc(s_small, 16)
            sp.dma_start(ln_g[:, :], ln[0].partition_broadcast(P)).then_inc(s_small, 16)
            sp.dma_start(ln_b[:, :], ln[1].partition_broadcast(P)).then_inc(s_small, 16)
            sp.wait_ge(s_yinit, 1)
            load(1)
            with sp.Fori(1, B - 1) as b:
                store(b - 1)
                sp.wait_ge(s_yinit, b + 1)
                load(b + 1)
            store(B - 2)
            store(B - 1)
            sp.wait_ge(s_store, 16 * B)

        @block.gpsimd
        def _(pool):
            make_identity(pool, ident, s_ident)

            def finish(b):
                pool.wait_ge(s_stats, b + 1)
                if not (isinstance(b, int) and b == 0):
                    pool.wait_ge(s_store, 16 * b)
                pool.nop(nofuse=True)
                layernorm_apply(pool, y, yo, mv, ve, rs, ntmp, ln_g, ln_b,
                                chain_on(pool, s_ln, b * LN_CHAIN), s_y_free).then_inc(s_fin, 1)

            pool.wait_ge(s_small, 16 * 4)
            finish(0)
            with pool.Fori(1, B - 1) as b:
                finish(b)
            finish(B - 1)

        @block.tensor
        def _(pe):
            def job(kind, arg, n, _, b, slot, prev):
                bank = job_ps[slot]
                last_h = n - (0 if prev == "h" else 2)
                if (kind, prev) == ("h", "xT"):
                    pe.wait_ge(s_job_done, n)
                elif (kind, arg) == ("y", 0):
                    pe.wait_ge(s_job_done, last_h - 1)
                elif (kind, arg) == ("h", 0):
                    pe.wait_ge(s_job_done, n - 2)
                elif b is not None or n >= NB:
                    pe.wait_ge(s_job_done, n - NB + 1)
                if kind in ("w1T", "w2T"):
                    i = n // 2
                    if n % 2 == 0:
                        pe.wait_ge(s_w[i % NSTAGE], 16 * (i // NSTAGE + 1))
                    tiles = [stage[i % NSTAGE][:, n % 2, c * P:(c + 1) * P] for c in range(KC)]
                elif kind == "xT":
                    nb = 0 if b is None else b + 1
                    pe.wait_ge(s_x, (nb + 1) * 16)
                    tiles = [x_raw[:, t, c * P:(c + 1) * P] for c in (2 * arg, 2 * arg + 1) for t in range(TB)]
                if kind in ("w1T", "w2T", "xT"):
                    for m, tile in enumerate(tiles):
                        mm = pe.transpose(bank[:, m * P:(m + 1) * P], tile, ident[:, :])
                elif kind == "h":
                    for c in range(2):
                        f = (2 * arg + c) * P
                        for kc in range(KC):
                            mm = matmul3(pe, bank[:, c * S:(c + 1) * S], [x[:, kc, f:f + P] for x in w1T],
                                         [x[:, kc, :] for x in xT], kc == 0, kc == KC - 1)
                else:
                    for fc in range(FC):
                        if arg == 0 and fc == FC - 2:
                            pe.wait_ge(s_job_done, last_h)
                        mm = matmul3(pe, bank[:, :], [x[:, fc, arg * P:(arg + 1) * P] for x in hT],
                                     [x[:, fc, :] for x in w2T], fc == 0, fc == FC - 1)
                mm.then_inc(s_job, 1)

            pe.wait_ge(s_ident, 2)
            run(pe, job, lambda b, n: None)

        def transposed(part, kind, arg):
            if kind == "w1T":
                return w1T[part][:, :, arg * P:(arg + 1) * P]
            if kind == "w2T":
                r, g = arg
                return w2T[part][:, g * KC:(g + 1) * KC, r * P:(r + 1) * P]
            return xT[part][:, 2 * arg:2 * arg + 2, :]

        def bank_view(bank, kind):
            return bank[:, :].rearrange("p (c f) -> p c f", c=2 if kind == "xT" else KC)

        @block.scalar
        def _(act):
            def job(kind, arg, n, _, b, slot, prev):
                if kind == "y":
                    return
                bank = job_ps[slot]
                act.wait_ge(s_job, n + 1)
                if kind == "h":
                    if isinstance(b, int) and (b, arg) == (0, 0):
                        act.wait_ge(s_small, 16 * 4)
                    for c in range(2):
                        m = 2 * arg + c
                        hi = act.activation(hidden[:, slot, c, :], bank[:, c * S:(c + 1) * S], ACT.Relu,
                                            bias=b1c[:, m:m + 1])
                else:
                    hi = act.activation(transposed(0, kind, arg), bank_view(bank, kind), ACT.Copy)
                hi.then_inc(s_job_hi, 1)

            run(act, job, lambda b, n: None)

        @block.vector
        def _(dve):
            def job(kind, arg, n, hi_jobs, b, slot, prev):
                bank = job_ps[slot]
                if kind == "y":
                    dve.wait_ge(s_job, n + 1)
                    lo = dve.tensor_tensor(y[:, arg, :], y[:, arg, :], bank[:, :], ALU.add)
                else:
                    if (kind, arg) == ("h", HJ // 2 - 1):
                        residual(b)
                    dve.wait_ge(s_job_hi, hi_jobs)
                    if kind == "h":
                        sl = slice(2 * arg, 2 * arg + 2)
                        dve.tensor_copy(hT[0][:, sl, :], hidden[:, slot, :, :]).then_inc(s_split, 1)
                        dve.wait_ge(s_split, b * HJ + arg + 1)
                        lo = dve.tensor_tensor(hT[1][:, sl, :], hidden[:, slot, :, :], hT[0][:, sl, :],
                                               ALU.subtract)
                    else:
                        lo = dve.tensor_tensor(transposed(1, kind, arg), bank_view(bank, kind),
                                               transposed(0, kind, arg), ALU.subtract)
                lo.then_inc(s_job_done, 1)

            def residual(b):
                if not (isinstance(b, int) and b == 0):
                    dve.wait_ge(s_y_free, b)
                else:
                    dve.wait_ge(s_small, 16 * 4)
                dve.tensor_tensor(y[:, :, :], x_raw[:, :, :], b2b[:, :].unsqueeze(1).to_broadcast([P, TB, D]),
                                  ALU.add).then_inc(s_yinit, 1)
                dve.wait_ge(s_yinit, b + 1)

            def statistics(b, jobs):
                dve.wait_ge(s_job_done, jobs)
                if not (isinstance(b, int) and b == 0):
                    dve.wait_ge(s_ln, b * LN_CHAIN)
                layernorm_stats(dve, y, stats, mv, s_bn, b, s_stats)

            run(dve, job, statistics)


def xattn_decoder(nc, x, ctx_1024, mask_k, mask_qk, w, out):
    B = x.shape[0]

    def between(n):
        return nc.dram_tensor(f"x{n}", x.shape, F32, kind="Internal").ap()

    x1, x2, x3 = between(1), between(2), between(3)
    attention_phase(nc, "a0_", B, x, ctx_1024, [w[f"L0_xattn_w{n}"] for n in "qkvo"],
                    x1, 64, norm_w=w["L0_xattn_norm_w"])
    attention_phase(nc, "a1_", B, x1, None, [w[f"L1_xattn_sa_w{n}"] for n in "qkvo"], x2, 32,
                    bias=[w[f"L1_xattn_sa_b{n}"] for n in "qkvo"], mask=mask_qk,
                    ln=(w["L1_xattn_ln1_g"], w["L1_xattn_ln1_b"]))
    attention_phase(nc, "a2_", B, x2, ctx_1024, [w[f"L1_xattn_ca_w{n}"] for n in "qkvo"], x3, 32,
                    bias=[w[f"L1_xattn_ca_b{n}"] for n in "qkvo"], mask=mask_k,
                    ln=(w["L1_xattn_ln2_g"], w["L1_xattn_ln2_b"]))
    ffn_phase(nc, "f_", B, x3, w["L1_xattn_ffn_w1"], w["L1_xattn_ffn_b1"], w["L1_xattn_ffn_w2"],
              w["L1_xattn_ffn_b2"], (w["L1_xattn_ln3_g"], w["L1_xattn_ln3_b"]), out)


def kernel(**inputs):
    import numpy as np
    import concourse.bacc as bacc
    from concourse.bass_utils import run_bass_kernel_spmd

    nc = bacc.Bacc("TRN2", target_bir_lowering=False, num_devices=1)
    arrays, args = {}, {}
    for name, value in inputs.items():
        a = np.ascontiguousarray(value)
        arrays[f"in_{name}"] = a
        args[name] = nc.dram_tensor(f"in_{name}", a.shape, mybir.dt.from_np(a.dtype), kind="ExternalInput").ap()
    out = nc.dram_tensor("out", inputs["x"].shape, F32, kind="ExternalOutput").ap()
    xattn_decoder(nc, args["x"], args["ctx_1024"], args["mask_Bx1x1xS2_if1"], args["mask_Bx1xSxS2_if1"], args, out)
    return run_bass_kernel_spmd(nc, [arrays], core_ids=[0]).results[0]["out"]
```

```python
from contextlib import ExitStack

import concourse.bass as bass
from concourse import mybir

ALU = mybir.AluOpType
ACT = mybir.ActivationFunctionType
AX = mybir.AxisListType
F32 = mybir.dt.float32
F32R = mybir.dt.float32r
I32 = mybir.dt.int32

P = 128
D = 512
S = 256
H = 16
KC = D // P
TB = S // P
UF = 256
CU = UF // P
RMS_EPS = 1e-6
LN_EPS = 1e-5
MASKED = -1e30
RSQRT_SEED = float(0x5F3759DF)
RSQRT_STEPS = 3
RSQRT_OPS = 1 + 4 * RSQRT_STEPS

PARTS = ((0, 0), (0, 1), (1, 0))


def matmul3(pe, out, lhs, rhs, first, last):
    for n, (a, b) in enumerate(PARTS):
        mm = pe.matmul(out, lhs[a], rhs[b], start=first and n == 0, stop=last and n == 2)
    return mm


def rsqrt_ops(eng, v, r, t, chain):
    chain(eng.tensor_scalar(r.bitcast(I32), v.bitcast(I32), -0.5, RSQRT_SEED, ALU.mult, ALU.add))
    for _ in range(RSQRT_STEPS):
        chain(eng.tensor_tensor(t, v, r, ALU.mult))
        chain(eng.tensor_tensor(t, t, r, ALU.mult))
        chain(eng.tensor_scalar(t, t, -0.5, 1.5, ALU.mult, ALU.add))
        chain(eng.tensor_tensor(r, r, t, ALU.mult))


def make_identity(pool, ident, s_ident):
    pool.memset(ident[:, :], 0.0).then_inc(s_ident, 1)
    pool.wait_ge(s_ident, 1)
    pool.affine_select(out=ident[:, :], in_=ident[:, :], compare_op=ALU.not_equal, fill=1.0,
                       base=0, pattern=[[-1, P]], channel_multiplier=1).then_inc(s_ident, 1)


def chain_on(eng, s, base):
    done = [0]

    def chain(ins):
        done[0] += 1
        ins.then_inc(s, 1)
        eng.wait_ge(s, base + done[0])
        eng.nop(nofuse=True)
    return chain


def row_stats(dve, y, stats, s_bn, t):
    dve.bn_stats(stats[:, t, :], y[:, t, :]).then_inc(s_bn, 1)


def row_mean_variance(dve, stats, mv, s_bn, n, s_stats):
    dve.wait_ge(s_bn, TB * (n + 1))
    dve.nop(nofuse=True)
    for t in range(TB):
        last = dve.bn_aggr(mv[:, t, :], stats[:, t, :])
    last.then_inc(s_stats, 1)


def last_layernorm(dve, B, y, yo, mv, ve, rs, ntmp, g, b, s_stats, s_store, s_ln, s_y_free):
    dve.wait_ge(s_stats, B)
    dve.wait_ge(s_store, 16 * (B - 1))
    return layernorm_apply(dve, y, yo, mv, ve, rs, ntmp, g, b, chain_on(dve, s_ln, (B - 1) * LN_CHAIN), s_y_free)


LN_CHAIN = 1 + RSQRT_OPS + TB + 1


def layernorm_apply(eng, y, yo, mv, ve, rs, tmp, g, b, chain, s_y_free):
    chain(eng.tensor_scalar(ve[:, :], mv[:, :, 1], LN_EPS, None, ALU.add))
    rsqrt_ops(eng, ve[:, :], rs[:, :], tmp[:, :], chain)
    for t in range(TB):
        chain(eng.tensor_scalar(yo[:, t, :], y[:, t, :], mv[:, t, 0:1], rs[:, t:t + 1], ALU.subtract, ALU.mult))
    eng.sem_inc(s_y_free, 1)
    chain(eng.tensor_tensor(yo[:, :, :], yo[:, :, :], g[:, :].unsqueeze(1).to_broadcast([P, TB, D]), ALU.mult))
    return eng.tensor_tensor(yo[:, :, :], yo[:, :, :], b[:, :].unsqueeze(1).to_broadcast([P, TB, D]), ALU.add)


class Ahead:
    SLOTS = 8

    def __init__(self, nc, ctx):
        self.buf = ctx.enter_context(nc.sbuf_tensor("ahead", [P, self.SLOTS, TB, D], F32))
        self.loaded = [ctx.enter_context(nc.semaphore(f"s_ahead{n}")) for n in range(self.SLOTS)]

    def load(self, sp, pieces):
        for n, piece in enumerate(pieces):
            sp.dma_start(self.buf[:, n, :, :], piece).then_inc(self.loaded[n], 16)


def row_pieces(weights):
    return [m[half * S:(half + 1) * S, :].rearrange("(t p) f -> p t f", p=P) for m in weights for half in range(2)]


def attention_phase(nc, tag, B, src, kv, w, dst, d, norm_w=None, bias=None, mask=None, ln=None,
                    ahead=None, use=1, next_pieces=()):
    DI = H * d
    U = DI // UF
    HU = UF // d
    assert U % 2 == 0 and B >= 3
    self_attention = kv is None
    transposed_weights = norm_w is None
    WQ, WK, WV, WO = (n * KC * DI for n in range(4))
    NW = 4 * KC * DI

    with ExitStack() as ctx:
        def sb(name, shape, dt):
            return ctx.enter_context(nc.sbuf_tensor(tag + name, shape, dt))

        def ps(name):
            return ctx.enter_context(nc.psum_tensor(tag + name, [P, 512], F32))

        def sem(name):
            return ctx.enter_context(nc.semaphore(tag + name))

        def pair(name, shape):
            return sb(name + "_hi", shape, F32R), sb(name + "_lo", shape, F32R)

        W = pair("w", [P, NW])
        xT = pair("xT", [P, KC, S])
        cT = xT if self_attention else pair("cT", [P, KC, S])
        q = pair("q", [P, 2, CU, S])
        k = pair("k", [P, 2, CU, S])
        v = pair("v", [P, 2, TB, (HU - 1) * P + d])
        pT = pair("pT", [P, 2, TB, S])
        oT = pair("oT", [P, CU, S])
        x_raw = sb("x_raw", [P, TB, D], F32)
        c_raw = sb("c_raw", [P, TB, D], F32)
        x_res = x_raw if HU == 4 else sb("x_res", [P, TB, D], F32)
        y = sb("y", [P, TB, D], F32)
        yo = sb("yo", [P, TB, D], F32)
        probs = sb("probs", [P, 2, TB, S], F32)
        ident = sb("ident", [P, P], F32)
        neg_max = sb("neg_max", [P, 2, TB], F32)
        row_sum = sb("row_sum", [P, 2, TB], F32)
        inv_sum = sb("inv_sum", [P, 2, TB], F32)
        if norm_w is not None:
            nw = sb("nw", [P, KC], F32)
            raw_max = sb("raw_max", [P, 2, TB], F32)
            sumsq = sb("sumsq", [P, TB], F32)
            rstd_next = sb("rstd_next", [P, TB], F32)
            rstd = sb("rstd", [P, TB], F32)
            rtmp = sb("rtmp", [P, TB], F32)
        if mask is not None:
            MT = 1 if mask.shape[2] == 1 else TB
            mask_raw = sb("mask_raw", [P, MT, S], I32)
            mask_add = sb("mask_add", [P, MT, S], F32)
        if bias is not None:
            bqk = sb("bqk", [P, 2, KC], F32)
            bo = sb("bo", [P, D], F32)
            bv_raw, ones_f = y[0:1, 0, :], y[0:1, 1, 0:P]
            bv = sb("bv_hi", [1, D], F32R), sb("bv_lo", [1, D], F32R)
            ones = sb("ones", [1, P], F32R)
        if ln is not None:
            ln_g = sb("ln_g", [P, D], F32)
            ln_b = sb("ln_b", [P, D], F32)
            stats = sb("stats", [P, TB, 6], F32)
            mv = sb("mv", [P, TB, 2], F32)
            ve = sb("ve", [P, TB], F32)
            rs = sb("rs", [P, TB], F32)
            ntmp = sb("ntmp", [P, TB], F32)

        scores_ps = [ps("scores0"), ps("scores1")]
        probsT_ps = [ps("probsT0"), ps("probsT1")]
        out_ps = [ps("out0"), ps("out1")]
        job_ps = [ps("job0"), ps("job1")]
        all_ps = job_ps + scores_ps + probsT_ps + out_ps

        s_x = sem("s_x")
        s_c = sem("s_c")
        s_m = sem("s_m")
        s_small = sem("s_small")
        NSTAGE = 3
        s_w = [sem(f"s_w{n}") for n in range(NSTAGE)]
        s_ident = sem("s_ident")
        s_whi = sem("s_whi")
        s_wlo = sem("s_wlo")
        s_bv = sem("s_bv")
        s_job = sem("s_job")
        s_job_hi = sem("s_job_hi")
        s_job_done = sem("s_job_done")
        s_scores = sem("s_scores")
        s_rawmax = sem("s_rawmax")
        s_max = sem("s_max")
        s_exp = sem("s_exp")
        s_probsT = sem("s_probsT")
        s_pT_hi = sem("s_pT_hi")
        s_pT_lo = sem("s_pT_lo")
        s_pv = sem("s_pv")
        s_zero = sem("s_zero")
        s_inv = sem("s_inv")
        s_norm = sem("s_norm")
        s_o_hi = sem("s_o_hi")
        s_o = sem("s_o")
        s_mask = sem("s_mask")
        s_sumsq = sem("s_sumsq")
        s_rms = sem("s_rms")
        s_rstd = sem("s_rstd")
        s_x_free = sem("s_x_free")
        s_bn = sem("s_bn")
        s_stats = sem("s_stats")
        s_ln = sem("s_ln")
        s_y_free = sem("s_y_free")
        s_fin = sem("s_fin")
        s_store = sem("s_store")

        def pieces(u, step, prev2=True, nxt=True):
            un = (u + 1) % U
            new = u == U - 1

            def halves(kind):
                return [(kind, un, 0)] if nxt else [], [(kind, un, 1)] if nxt else []

            (q0, q1), (k0, k1), (v0, v1) = halves("q"), halves("k"), halves("v")
            wo0, wo1 = ([("wo", (t, (u - 2) % U), 1)] if prev2 else [] for t in range(TB))
            load = [(kind, n, 1) for kind in (("xT",) if self_attention else ("xT", "cT"))
                    for n in range(2)] if nxt and new else []
            t0, t1, t2, t3 = (load[n:n + 1] for n in range(4))
            if HU == 4:
                table = ([(t0, wo0 + t1), (t2 + q0, q1 + t3), (wo1 + k0, k1), (v0, v1)] if load else
                         [(wo0, wo1), (q0, q1), (k0, k1), (v0, v1)])
            else:
                q_late = bool(t3)
                table = [(wo0, t0), (wo1, t1), (t2, t3 or q0), (q0 + q1 if q_late else q1, []),
                         ([], k0), (k1, []), (v0, []), (v1, [])]
            return table[step]

        def ending(part):
            return [(kind, arg) for kind, arg, half in part if half == 1]

        def jobs(u, step, **which):
            return [j for part in pieces(u, step, **which) for j in ending(part)]

        def load_jobs():
            return ([] if self_attention else [("cT", 0), ("cT", 1)]) + [("xT", 0), ("xT", 1)]

        def exist(seg, u):
            first, last = seg == "first", seg == "last"
            return dict(prev2=not (first and u < 2), nxt=not (last and u == U - 1))

        def seg_jobs(seg):
            return [j for u in range(U) for st in range(HU) for j in jobs(u, st, **exist(seg, u))]

        weight_jobs = [("wT", (n, r)) for n in range(4) for r in range(D // P)] if transposed_weights else []
        pro_jobs = weight_jobs + load_jobs() + [("q", 0), ("k", 0), ("v", 0)]
        FINISH = (1, 0) if HU == 4 else (1, 1)
        STATISTICS = (2, 3, 4)
        SQUARES = (U - 1, 1)
        X_FREE = (2, 0) if HU == 4 else (0, 2)
        epi_jobs = [("wo", (0, U - 2)), ("wo", (1, U - 2)), ("wo", (0, U - 1)), ("wo", (1, U - 1))]

        def has_hi(kind):
            return kind != "wo"

        def counts(js):
            return len(js), sum(has_hi(kind) for kind, _ in js)

        N_PRO, N_FIRST, N_MID, N_LAST = (counts(x) for x in
                                         (pro_jobs, seg_jobs("first"), seg_jobs("mid"), seg_jobs("last")))
        assert N_MID[0] % 2 == 0

        class Place:

            def __init__(self, b, all_jobs, hi_jobs, parity, prev=None):
                self.b, self.base, self.hi_base, self.parity, self.prev = b, all_jobs, hi_jobs, parity, prev
                self.n = self.n_hi = self.slot_start = 0
                self.bank = None

            def next(self, kind):
                if kind == "wT":
                    bank = all_ps[self.n % len(all_ps)]
                else:
                    bank = job_ps[(self.parity + self.n) % 2]
                self.n += 1
                self.n_hi += has_hi(kind)
                self.prev = kind
                return bank

            @property
            def job(self):
                return self.base + self.n

            @property
            def hi_job(self):
                return self.hi_base + self.n_hi

        def run(eng, prologue, step, epilogue):
            def entry(seg, place):
                for u in range(U):
                    for st in range(HU):
                        step(place, seg, u, st)

            prologue(Place(None, 0, 0, 0))
            entry("first", Place(0, N_PRO[0], N_PRO[1], N_PRO[0]))
            b0 = tuple(N_PRO[n] + N_FIRST[n] for n in range(2))
            with eng.Fori(1, B - 1) as b:
                entry("mid", Place(b, (b - 1) * N_MID[0] + b0[0], (b - 1) * N_MID[1] + b0[1], b0[0]))
            b1 = tuple(b0[n] + (B - 2) * N_MID[n] for n in range(2))
            entry("last", Place(B - 1, b1[0], b1[1], b1[0]))
            e = tuple(b1[n] + N_LAST[n] for n in range(2))
            epilogue(Place(B, e[0], e[1], e[0], prev="v"))

        def head_wait(eng, s, seg, place, h, lag, count):
            if seg == "first" and h - lag + 1 <= 0:
                return
            eng.wait_ge(s, place.b * H + (h - lag + 1) if count is None else count)

        def unit_count(place, u):
            return place.b * U + (u + 1)

        def v_window(j):
            return j * P - j * d % P

        def v_columns(part, u):
            return v[part][:, u % 2, :, :].rearrange("p t (n e) -> p t n e", e=d)[:, :, ::P // d, :]

        def wT_out(part, n, r):
            return W[part][:, n * KC * D:(n + 1) * KC * D].rearrange("p (c f) -> p c f", c=KC)[:, :, r * P:(r + 1) * P]

        stage = [y[:, :, :], yo[:, :, :], probs[:, :, :, :].rearrange("p n t s -> p n (t s)")]

        PRO_PIECES = 4
        UNIT_PIECES = [("q", 0), ("k", 0), ("v", 0)] + [
            (kind, u + (kind != "wo")) for u in range(U) for kind in ("q", "k", "v", "wo")
            if kind == "wo" or u + 1 < U]
        PIECE_STAGE = [0, 1, 2] + [(0 if i % 2 and i < PRO_PIECES + 2 * HU else 1) for i in range(3, len(UNIT_PIECES))]

        def pieces_in_step(u, j):
            i = PRO_PIECES + u * HU + j
            return [i] if not transposed_weights and i < len(UNIT_PIECES) else []

        def piece_load(i):
            return 16 * PIECE_STAGE[:i + 1].count(PIECE_STAGE[i])

        def piece_view(part, i):
            kind, u = UNIT_PIECES[i]
            if kind == "wo":
                return W[part][:, WO + u * CU * D:WO + (u + 1) * CU * D].rearrange("p (c f) -> p c f", c=CU)
            off = {"q": WQ, "k": WK, "v": WV}[kind]
            return W[part][:, off:off + KC * DI].rearrange("p (c f) -> p c f", c=KC)[:, :, u * UF:(u + 1) * UF]

        def piece_raw(i):
            raw = stage[PIECE_STAGE[i]].rearrange("p t f -> p (t f)")
            return raw.rearrange("p (c f) -> p c f", c=CU if UNIT_PIECES[i][0] == "wo" else KC)

        block = ctx.enter_context(nc.Block())

        @block.sync
        def _(sp):
            x_v = src.rearrange("b (t p) f -> b p t f", p=P)
            dst_v = dst.rearrange("b (t p) f -> b p t f", p=P)

            def load_x(b):
                sp.dma_start(x_raw[:, :, :], x_v[b]).then_inc(s_x, 16)
                if mask is not None:
                    if mask.shape[2] == 1:
                        sp.dma_start(mask_raw[:, 0, :], mask[b, 0, 0].partition_broadcast(P)).then_inc(s_m, 16)
                    else:
                        m_v = mask.rearrange("b a (t p) k -> (b a) p t k", p=P)
                        sp.dma_start(mask_raw[:, :, :], m_v[b]).then_inc(s_m, 16)

            def load_c(b):
                if not self_attention:
                    sp.dma_start(c_raw[:, :, :], kv.rearrange("b (t p) f -> b p t f", p=P)[b]).then_inc(s_c, 16)

            def store(b):
                sp.wait_ge(s_fin, b + 1)
                sp.nop(nofuse=True)
                sp.dma_start(dst_v[b], yo[:, :, :]).then_inc(s_store, 16)

            AHEAD = 2

            def load_piece(i):
                if PIECE_STAGE[i] in PIECE_STAGE[:i]:
                    before = max(n for n in range(i) if PIECE_STAGE[n] == PIECE_STAGE[i])
                    sp.wait_ge(s_wlo, before + 1)
                kind, u = UNIT_PIECES[i]
                if kind == "wo":
                    piece = w[3][u * UF:(u + 1) * UF, :].rearrange("(c p) f -> p c f", p=P)
                else:
                    n = ("q", "k", "v").index(kind)
                    piece = w[n][:, u * UF:(u + 1) * UF].rearrange("(c p) f -> p c f", p=P)
                sp.dma_start(piece_raw(i), piece).then_inc(s_w[PIECE_STAGE[i]], 16)

            if not transposed_weights:
                load_c(0)
                load_x(0)
            if norm_w is not None:
                with nc.allow_non_contiguous_dma("a column per chunk"):
                    sp.dma_start(nw[:, :], norm_w.rearrange("(c p) -> p c", p=P)).then_inc(s_small, 16)
            if transposed_weights:
                if use == 1:
                    ahead.load(sp, row_pieces(w))
                load_c(0)
                load_x(0)
            else:
                for i in range(PRO_PIECES + AHEAD):
                    load_piece(i)
            if bias is not None:
                with nc.allow_non_contiguous_dma("a column per chunk"):
                    sp.dma_start(bqk[:, 0, :], bias[0].rearrange("(c p) -> p c", p=P)).then_inc(s_small, 16)
                    sp.dma_start(bqk[:, 1, :], bias[1].rearrange("(c p) -> p c", p=P)).then_inc(s_small, 16)
                sp.dma_start(bv_raw, bias[2].rearrange("(a f) -> a f", a=1)).then_inc(s_small, 16)
                sp.dma_start(bo[:, :], bias[3].partition_broadcast(P)).then_inc(s_small, 16)
                sp.dma_start(ln_g[:, :], ln[0].partition_broadcast(P)).then_inc(s_small, 16)
                sp.dma_start(ln_b[:, :], ln[1].partition_broadcast(P)).then_inc(s_small, 16)

            def prologue(place):
                if transposed_weights:
                    sp.wait_ge(s_job, len(weight_jobs))
                    ahead.load(sp, next_pieces)
                for kind, _ in pro_jobs:
                    place.next(kind)

            def step(place, seg, u, j):
                if u == 0 and j == 0 and seg != "last" and not self_attention:
                    sp.wait_ge(s_job, place.job)
                    sp.nop(nofuse=True)
                    if norm_w is not None:
                        sp.wait_ge(s_sumsq, place.b + 1)
                        sp.nop(nofuse=True)
                    load_c(place.b + 1)
                for kind, _ in jobs(u, j, **exist(seg, u)):
                    place.next(kind)
                if seg == "first":
                    for i in pieces_in_step(u, j):
                        if i + AHEAD < len(UNIT_PIECES):
                            load_piece(i + AHEAD)
                if (u, j) == X_FREE and seg != "last":
                    if x_res is x_raw:
                        sp.wait_ge(s_job_done, place.job)
                    else:
                        sp.wait_ge(s_x_free, place.b + 1)
                    sp.nop(nofuse=True)
                    load_x(place.b + 1)
                if (u, j) == FINISH and seg != "first":
                    store(place.b - 1)

            def epilogue(place):
                store(B - 1)
                sp.wait_ge(s_store, 16 * B)

            run(sp, prologue, step, epilogue)

        @block.gpsimd
        def _(pool):
            make_identity(pool, ident, s_ident)
            for part in v:
                pool.memset(part[:, :, :, :].bitcast(F32), 0.0).then_inc(s_zero, 1)

            def finish(place, b):
                if ln is None:
                    pool.wait_ge(s_job_done, place.job)
                else:
                    pool.wait_ge(s_stats, b + 1)
                if not (isinstance(b, int) and b == 0):
                    pool.wait_ge(s_store, 16 * b)
                pool.nop(nofuse=True)
                if ln is None:
                    pool.tensor_copy(yo[:, :, :], y[:, :, :]).then_inc(s_fin, 1)
                else:
                    layernorm_apply(pool, y, yo, mv, ve, rs, ntmp, ln_g, ln_b,
                                    chain_on(pool, s_ln, b * LN_CHAIN), s_y_free).then_inc(s_fin, 1)

            def inverse_rms(nb):
                pool.wait_ge(s_sumsq, nb + 1)
                if not (isinstance(nb, int) and nb == 0):
                    pool.wait_ge(s_rstd, nb)
                pool.nop(nofuse=True)
                rsqrt_ops(pool, sumsq[:, :], rstd_next[:, :], rtmp[:, :], chain_on(pool, s_rms, nb * RSQRT_OPS))

            def residual(place):
                pool.wait_ge(s_x, (place.b + 1) * 16)
                pool.wait_ge(s_job_done, place.job)
                pool.nop(nofuse=True)
                pool.tensor_tensor(x_res[:, :, :], x_raw[:, :, :], bo[:, :].unsqueeze(1).to_broadcast([P, TB, D]),
                                   ALU.add).then_inc(s_x_free, 1)

            def prologue(place):
                for kind, _ in pro_jobs:
                    place.next(kind)
                if norm_w is not None:
                    inverse_rms(0)

            def step(place, seg, u, j):
                for kind, _ in jobs(u, j, **exist(seg, u)):
                    place.next(kind)
                if (u, j) == FINISH and seg != "first":
                    finish(place, place.b - 1)
                if (u, j) == X_FREE and x_res is not x_raw:
                    residual(place)
                if norm_w is not None and (u, j) == SQUARES and seg != "last":
                    inverse_rms(place.b + 1)

            def epilogue(place):
                for kind, _ in epi_jobs:
                    place.next(kind)
                if ln is None:
                    finish(place, B - 1)

            if bias is not None:
                pool.wait_ge(s_small, 16 * 6)
                pool.sem_inc(s_y_free, 1)
            run(pool, prologue, step, epilogue)

        @block.tensor
        def _(pe):
            def transposes(bank, tiles):
                for n, t in enumerate(tiles):
                    tr = pe.transpose(bank[:, n * P:(n + 1) * P], t, ident[:, :])
                return tr

            def piece(place, kind, arg, half):
                if kind in ("q", "k", "v"):
                    first, last = half == 0, half == 1
                else:
                    first = last = True
                if first:
                    start_job(place, kind)
                mm = run_job(place, place.bank, kind, arg, (half,) if kind in ("q", "k", "v") else (0, 1))
                if last:
                    mm.then_inc(s_job, 1)

            def job(place, kind, arg):
                start_job(place, kind)
                run_job(place, place.bank, kind, arg, (0, 1)).then_inc(s_job, 1)

            def start_job(place, kind):
                n, prev = place.job, place.prev
                place.bank = place.next(kind)
                if (kind, prev) in (("q", "xT"), ("k", "cT")):
                    pe.wait_ge(s_job_done, n)
                elif kind == "wT":
                    if n >= len(all_ps):
                        pe.wait_ge(s_job_done, n - len(all_ps) + 1)
                elif place.b is not None or n >= 2:
                    pe.wait_ge(s_job_done, n - 1)

            def run_job(place, bank, kind, arg, halves):
                if kind == "wT":
                    wi, r = arg
                    i = wi * 2 + r // 2
                    if r % 2 == 0:
                        pe.wait_ge(ahead.loaded[i], 16 * use)
                    mm = transposes(bank, [ahead.buf[:, i, r % 2, c * P:(c + 1) * P] for c in range(KC)])
                elif kind in ("xT", "cT"):
                    raw = x_raw if kind == "xT" else c_raw
                    nb = 0 if place.b is None else place.b + 1
                    pe.wait_ge(s_x if kind == "xT" else s_c, (nb + 1) * 16)
                    mm = transposes(bank, [raw[:, t, c * P:(c + 1) * P] for c in (2 * arg, 2 * arg + 1)
                                           for t in range(TB)])
                elif kind in ("q", "k"):
                    a = xT if kind == "q" else cT
                    off = WQ if kind == "q" else WK
                    weight_wait(place, kind, arg)
                    for c in halves:
                        for kc in range(KC):
                            f = off + kc * DI + arg * UF + c * P
                            mm = matmul3(pe, bank[:, c * S:(c + 1) * S], [x[:, f:f + P] for x in W],
                                         [x[:, kc, :] for x in a], kc == 0, kc == KC - 1)
                elif kind == "v":
                    weight_wait(place, kind, arg)
                    for t in halves:
                        out = bank[:, t * UF:(t + 1) * UF]
                        for kc in range(KC):
                            f = WV + kc * DI + arg * UF
                            mm = matmul3(pe, out, [x[:, kc, t * P:(t + 1) * P] for x in cT],
                                         [x[:, f:f + UF] for x in W], kc == 0, kc == KC - 1 and bias is None)
                        if bias is not None:
                            pe.matmul(out, ones[:, :], bv[0][:, arg * UF:(arg + 1) * UF], start=False, stop=False)
                            mm = pe.matmul(out, ones[:, :], bv[1][:, arg * UF:(arg + 1) * UF], start=False, stop=True)
                else:
                    t, u = arg
                    weight_wait(place, kind, u)
                    if t == 0:
                        pe.wait_ge(s_o, unit_count(place, u - U if u >= U - 2 else u))
                    for c in range(CU):
                        f = WO + (u * CU + c) * D
                        mm = matmul3(pe, bank[:, :], [x[:, c, t * P:(t + 1) * P] for x in oT],
                                     [x[:, f:f + D] for x in W], c == 0, c == CU - 1)
                return mm

            def weight_wait(place, kind, u):
                first_use = place.b is None or isinstance(place.b, int) and place.b == 0 or kind == "wo" and u >= U - 2
                if not transposed_weights and first_use:
                    pe.wait_ge(s_wlo, UNIT_PIECES.index((kind, u)) + 1)

            def scores(place, seg, u, j):
                h = u * HU + j
                if j == 0:
                    pe.wait_ge(s_job_done, place.job - 1)
                head_wait(pe, s_exp, seg, place, h, 2, None)
                bank = scores_ps[h % 2]
                c, r = j * d // P, j * d % P
                for t in range(TB):
                    mm = matmul3(pe, bank[:, t * S:(t + 1) * S],
                                 [x[r:r + d, u % 2, c, t * P:(t + 1) * P] for x in q],
                                 [x[r:r + d, u % 2, c, :] for x in k], True, True)
                mm.then_inc(s_scores, 1)

            def transpose_probs(place, seg, h):
                head_wait(pe, s_norm, seg, place, h, 0, None)
                head_wait(pe, s_pT_lo, seg, place, h, 2, None)
                hb = h % 2
                transposes(probsT_ps[hb], [probs[:, hb, t, kb * P:(kb + 1) * P] for kb in range(TB)
                                           for t in range(TB)]).then_inc(s_probsT, 1)

            def attend(place, seg, h, v_jobs):
                j, ub = h % HU, (h // HU) % 2
                if j == 0:
                    pe.wait_ge(s_job_done, v_jobs)
                    if not (seg == "first" and h < 2 * HU):
                        pe.wait_ge(s_o, unit_count(place, h // HU) - 2)
                head_wait(pe, s_pT_lo, seg, place, h, 0, None)
                c, r = j * d // P, j * d % P
                for kb in range(TB):
                    mm = matmul3(pe, out_ps[ub][:, c * S:(c + 1) * S],
                                 [x[:, ub, kb, v_window(j):v_window(j) + P] for x in v],
                                 [x[:, h % 2, kb, :] for x in pT],
                                 r == 0 and kb == 0, r == P - d and kb == TB - 1)
                mm.then_inc(s_pv, 1)

            def prologue(place):
                pe.wait_ge(s_ident, 2)
                for kind, arg in pro_jobs:
                    if bias is not None and kind == "v":
                        pe.wait_ge(s_bv, 4)
                    job(place, kind, arg)

            def step(place, seg, u, j):
                h = u * HU + j
                if j == 0:
                    place.slot_start = place.job
                early, late = pieces(u, j, **exist(seg, u))
                scores(place, seg, u, j)
                if h >= 2 or seg != "first":
                    transpose_probs(place, seg, h - 2)
                for kind, arg, half in early:
                    piece(place, kind, arg, half)
                if h >= 3 or seg != "first":
                    attend(place, seg, h - 3, place.slot_start)
                for kind, arg, half in late:
                    piece(place, kind, arg, half)

            def epilogue(place):
                transpose_probs(place, "epi", -2)
                attend(place, "epi", -3, None)
                transpose_probs(place, "epi", -1)
                attend(place, "epi", -2, None)
                attend(place, "epi", -1, None)
                for kind, arg in epi_jobs:
                    job(place, kind, arg)

            run(pe, prologue, step, epilogue)

        @block.scalar
        def _(act):
            def job(place, kind, arg):
                bank = place.next(kind)
                if not has_hi(kind):
                    return
                act.wait_ge(s_job, place.job)
                if kind == "wT":
                    hi = act.activation(wT_out(0, *arg), bank[:, :].rearrange("p (c f) -> p c f", c=KC), ACT.Copy)
                elif kind in ("xT", "cT"):
                    a = xT if kind == "xT" else cT
                    hi = act.activation(a[0][:, 2 * arg:2 * arg + 2, :],
                                        bank[:, :].rearrange("p (c t) -> p c t", c=2), ACT.Copy)
                elif kind in ("q", "k"):
                    out = (q if kind == "q" else k)[0][:, arg % 2, :, :]
                    if bias is None:
                        hi = act.activation(out, bank[:, :].rearrange("p (c t) -> p c t", c=CU), ACT.Copy)
                    else:
                        for c in range(CU):
                            b_col = bqk[:, int(kind == "k"), arg * CU + c:arg * CU + c + 1]
                            hi = act.activation(out[:, c, :], bank[:, c * S:(c + 1) * S], ACT.Identity, bias=b_col)
                else:
                    if place.b is None:
                        act.wait_ge(s_zero, 2)
                    hi = act.activation(v_columns(0, arg), bank[:, :].rearrange("p (t h e) -> p t h e", t=TB, h=HU),
                                        ACT.Copy)
                hi.then_inc(s_job_hi, 1)

            def weights_hi(i):
                act.wait_ge(s_w[PIECE_STAGE[i]], piece_load(i))
                out, raw = piece_view(0, i), piece_raw(i)
                if UNIT_PIECES[i][0] == "q":
                    for c in range(KC):
                        hi = act.activation(out[:, c, :], raw[:, c, :], ACT.Copy, scale=nw[:, c:c + 1])
                else:
                    hi = act.activation(out, raw, ACT.Copy)
                hi.then_inc(s_whi, 1)

            def exps(place, seg, u, j):
                h = u * HU + j
                head_wait(act, s_max, seg, place, h, 0, None)
                head_wait(act, s_probsT, seg, place, h, 2, None)
                for t in range(TB):
                    scale = rstd[:, t:t + 1] if norm_w is not None else -1.0
                    e = act.activation(probs[:, h % 2, t, :], scores_ps[h % 2][:, t * S:(t + 1) * S], ACT.Exp,
                                       bias=neg_max[:, h % 2, t:t + 1], scale=scale,
                                       accum_out=row_sum[:, h % 2, t:t + 1])
                e.then_inc(s_exp, 1)

            def normalise(place, seg, h):
                head_wait(act, s_inv, seg, place, h, 0, None)
                for t in range(TB):
                    n = act.activation(probs[:, h % 2, t, :], probs[:, h % 2, t, :], ACT.Copy,
                                       scale=inv_sum[:, h % 2, t:t + 1])
                n.then_inc(s_norm, 1)

            def unit_output(place, u):
                n = unit_count(place, u)
                act.wait_ge(s_pv, n * HU)
                act.wait_ge(s_job, place.job)
                act.activation(oT[0][:, :, :], out_ps[u % 2][:, :].rearrange("p (c t) -> p c t", c=CU),
                               ACT.Copy).then_inc(s_o_hi, 1)

            def probsT_hi(place, seg, h):
                head_wait(act, s_probsT, seg, place, h, 0, None)
                head_wait(act, s_pv, seg, place, h, 2, None)
                act.activation(pT[0][:, h % 2, :, :], probsT_ps[h % 2][:, :].rearrange("p (k t) -> p k t", k=TB),
                               ACT.Copy).then_inc(s_pT_hi, 1)

            def prologue(place):
                if not transposed_weights:
                    act.wait_ge(s_small, 16)
                for kind, arg in pro_jobs:
                    if not transposed_weights and (kind, arg) in UNIT_PIECES:
                        weights_hi(UNIT_PIECES.index((kind, arg)))
                    if bias is not None and (kind, arg) == ("q", 0):
                        act.wait_ge(s_bv, 1)
                        act.wait_ge(s_small, 16 * 6)
                        act.activation(ones[:, :], ones_f, ACT.Copy).then_inc(s_bv, 1)
                        act.activation(bv[0][:, :], bv_raw, ACT.Copy).then_inc(s_bv, 1)
                    job(place, kind, arg)
                if not transposed_weights:
                    for i in range(3, PRO_PIECES):
                        weights_hi(i)

            def step(place, seg, u, j):
                h = u * HU + j
                early, late = pieces(u, j, **exist(seg, u))
                if h >= 1 or seg != "first":
                    normalise(place, seg, h - 1)
                if h >= 2 or seg != "first":
                    probsT_hi(place, seg, h - 2)
                exps(place, seg, u, j)
                if j == 3 and (u >= 1 or seg != "first"):
                    unit_output(place, u - 1)
                if seg == "first":
                    for i in pieces_in_step(u, j):
                        weights_hi(i)
                for kind, arg in ending(early):
                    job(place, kind, arg)
                for kind, arg in ending(late):
                    job(place, kind, arg)

            def epilogue(place):
                normalise(place, "epi", -1)
                probsT_hi(place, "epi", -2)
                probsT_hi(place, "epi", -1)
                for kind, arg in epi_jobs:
                    if (kind, arg) == ("wo", (0, U - 1)):
                        unit_output(place, -1)
                    job(place, kind, arg)

            run(act, prologue, step, epilogue)

        @block.vector
        def _(dve):
            def job(place, kind, arg):
                n = place.job
                bank = place.next(kind)
                if has_hi(kind):
                    dve.wait_ge(s_job_hi, place.hi_job)
                if kind == "wT":
                    lo = dve.tensor_tensor(wT_out(1, *arg), bank[:, :].rearrange("p (c f) -> p c f", c=KC),
                                           wT_out(0, *arg), ALU.subtract)
                elif kind in ("xT", "cT"):
                    a = xT if kind == "xT" else cT
                    sl = slice(2 * arg, 2 * arg + 2)
                    lo = dve.tensor_tensor(a[1][:, sl, :], bank[:, :].rearrange("p (c t) -> p c t", c=2),
                                           a[0][:, sl, :], ALU.subtract)
                elif kind in ("q", "k"):
                    a = q if kind == "q" else k
                    hi, out = a[0][:, arg % 2, :, :], a[1][:, arg % 2, :, :]
                    if bias is None:
                        lo = dve.tensor_tensor(out, bank[:, :].rearrange("p (c t) -> p c t", c=CU), hi, ALU.subtract)
                    else:
                        for c in range(CU):
                            b_col = bqk[:, int(kind == "k"), arg * CU + c:arg * CU + c + 1]
                            lo = dve.scalar_tensor_tensor(out=out[:, c, :], in0=bank[:, c * S:(c + 1) * S],
                                                          scalar=b_col, in1=hi[:, c, :], op0=ALU.add,
                                                          op1=ALU.subtract)
                elif kind == "v":
                    lo = dve.tensor_tensor(v_columns(1, arg), bank[:, :].rearrange("p (t h e) -> p t h e", t=TB, h=HU),
                                           v_columns(0, arg), ALU.subtract)
                else:
                    t, unit = arg
                    if unit == 0 and t == 0:
                        b = place.b if HU == 4 else place.b - 1
                        if not (isinstance(b, int) and b == 0):
                            if ln is None:
                                dve.wait_ge(s_fin, b)
                            else:
                                dve.wait_ge(s_y_free, b + 1)
                    if unit == 0 and t == 0 and x_res is not x_raw:
                        dve.wait_ge(s_x_free, place.b)
                    dve.wait_ge(s_job, place.job)
                    dve.wait_ge(s_job_done, n)
                    lo = dve.tensor_tensor(y[:, t, :], (x_res if unit == 0 else y)[:, t, :], bank[:, :], ALU.add)
                lo.then_inc(s_job_done, 1)

            def sum_squares(nb):
                if not (isinstance(nb, int) and nb == 0):
                    dve.wait_ge(s_rms, nb * RSQRT_OPS)
                dve.wait_ge(s_x, (nb + 1) * 16)
                dve.nop(nofuse=True)
                for t in range(TB):
                    total = dve.tensor_tensor_reduce(out=c_raw[:, t, :], in0=x_raw[:, t, :], in1=x_raw[:, t, :],
                                                     scale=1.0 / D, scalar=RMS_EPS, op0=ALU.mult, op1=ALU.add,
                                                     accum_out=sumsq[:, t:t + 1])
                total.then_inc(s_sumsq, 1)

            def weights_lo(i):
                dve.wait_ge(s_w[PIECE_STAGE[i]], piece_load(i))
                dve.wait_ge(s_whi, i + 1)
                hi, out, raw = piece_view(0, i), piece_view(1, i), piece_raw(i)
                if UNIT_PIECES[i][0] == "q":
                    for c in range(KC):
                        lo = dve.scalar_tensor_tensor(out=out[:, c, :], in0=raw[:, c, :], scalar=nw[:, c:c + 1],
                                                      in1=hi[:, c, :], op0=ALU.mult, op1=ALU.subtract)
                else:
                    lo = dve.tensor_tensor(out, raw, hi, ALU.subtract)
                lo.then_inc(s_wlo, 1)

            def convert_mask(b):
                if not (isinstance(b, int) and b == 0):
                    dve.wait_ge(s_max, b * H)
                dve.wait_ge(s_m, (b + 1) * 16)
                dve.tensor_scalar(mask_add[:, :, :], mask_raw[:, :, :], 0.0, MASKED, ALU.is_equal,
                                  ALU.mult).then_inc(s_mask, 1)

            def maxima(place, seg, u, j):
                h = u * HU + j
                hb = h % 2
                if h == 0:
                    if norm_w is not None:
                        if seg != "first":
                            dve.wait_ge(s_exp, place.b * H)
                        dve.wait_ge(s_rms, (place.b + 1) * RSQRT_OPS)
                        dve.tensor_copy(rstd[:, :], rstd_next[:, :]).then_inc(s_rstd, 1)
                        dve.wait_ge(s_rstd, place.b + 1)
                    if mask is not None:
                        dve.wait_ge(s_mask, place.b + 1)
                head_wait(dve, s_scores, seg, place, h, 0, None)
                bank = scores_ps[hb]
                if norm_w is not None:
                    dve.tensor_reduce(raw_max[:, hb, :], bank[:, :].rearrange("p (t k) -> p t k", t=TB), AX.X,
                                      ALU.max, negate=True).then_inc(s_rawmax, 1)
                    head_wait(dve, s_rawmax, seg, place, h, 0, None)
                    dve.tensor_tensor(neg_max[:, hb, :], raw_max[:, hb, :], rstd[:, :],
                                      ALU.mult).then_inc(s_max, 1)
                else:
                    dve.nop(nofuse=True)
                    for t in range(TB):
                        m = dve.tensor_tensor_reduce(out=bank[:, t * S:(t + 1) * S], in0=bank[:, t * S:(t + 1) * S],
                                                     in1=mask_add[:, t % MT, :], scale=-float(d) ** -0.5, scalar=3e38,
                                                     op0=ALU.add, op1=ALU.min, accum_out=neg_max[:, hb, t:t + 1])
                    m.then_inc(s_max, 1)

            def probsT_lo(place, seg, h):
                head_wait(dve, s_pT_hi, seg, place, h, 0, None)
                hb = h % 2
                dve.tensor_tensor(pT[1][:, hb, :, :], probsT_ps[hb][:, :].rearrange("p (k t) -> p k t", k=TB),
                                  pT[0][:, hb, :, :], ALU.subtract).then_inc(s_pT_lo, 1)

            def inverse(place, seg, h):
                head_wait(dve, s_exp, seg, place, h, 0, None)
                dve.reciprocal(inv_sum[:, h % 2, :], row_sum[:, h % 2, :]).then_inc(s_inv, 1)

            def unit_output(place, u):
                dve.wait_ge(s_o_hi, unit_count(place, u))
                dve.tensor_tensor(oT[1][:, :, :], out_ps[u % 2][:, :].rearrange("p (c t) -> p c t", c=CU),
                                  oT[0][:, :, :], ALU.subtract).then_inc(s_o, 1)

            def statistics(place, b, part):
                if part < TB:
                    if part == 0:
                        dve.wait_ge(s_job_done, place.job)
                        dve.nop(nofuse=True)
                    row_stats(dve, y, stats, s_bn, part)
                else:
                    if not (isinstance(b, int) and b == 0):
                        dve.wait_ge(s_ln, b * LN_CHAIN)
                    row_mean_variance(dve, stats, mv, s_bn, b, s_stats)

            def prologue(place):
                if not transposed_weights:
                    dve.wait_ge(s_small, 16)
                for kind, arg in pro_jobs:
                    if mask is not None and (kind, arg) == ("k", 0):
                        convert_mask(0)
                    if norm_w is not None and (kind, arg) == ("q", 0):
                        sum_squares(0)
                    if not transposed_weights and (kind, arg) in UNIT_PIECES:
                        weights_lo(UNIT_PIECES.index((kind, arg)))
                    if bias is not None and (kind, arg) == ("q", 0):
                        dve.memset(ones_f, 1.0).then_inc(s_bv, 1)
                        dve.wait_ge(s_bv, 3)
                        dve.wait_ge(s_small, 16 * 6)
                        dve.tensor_tensor(bv[1][:, :], bv_raw, bv[0][:, :], ALU.subtract).then_inc(s_bv, 1)
                    job(place, kind, arg)
                if not transposed_weights:
                    for i in range(3, PRO_PIECES):
                        weights_lo(i)

            def step(place, seg, u, j):
                h = u * HU + j
                early, late = pieces(u, j, **exist(seg, u))
                if h >= 1 or seg != "first":
                    inverse(place, seg, h - 1)
                maxima(place, seg, u, j)
                if h >= 2 or seg != "first":
                    probsT_lo(place, seg, h - 2)
                if mask is not None and (u, j) == (U - 1, HU - 1) and seg != "last":
                    convert_mask(place.b + 1)
                if j == 3 and (u >= 1 or seg != "first"):
                    unit_output(place, u - 1)
                if seg == "first":
                    for i in pieces_in_step(u, j):
                        weights_lo(i)
                for kind, arg in ending(early):
                    job(place, kind, arg)
                for kind, arg in ending(late):
                    job(place, kind, arg)
                if u == 1 and j in STATISTICS and seg != "first" and ln is not None:
                    statistics(place, place.b - 1, STATISTICS.index(j))
                if norm_w is not None and (u, j) == SQUARES and seg != "last":
                    sum_squares(place.b + 1)

            def epilogue(place):
                inverse(place, "epi", -1)
                probsT_lo(place, "epi", -2)
                probsT_lo(place, "epi", -1)
                for kind, arg in epi_jobs:
                    if (kind, arg) == ("wo", (0, U - 1)):
                        unit_output(place, -1)
                    job(place, kind, arg)
                if ln is not None:
                    for part in range(TB + 1):
                        statistics(place, B - 1, part)
                    last_layernorm(dve, B, y, yo, mv, ve, rs, ntmp, ln_g, ln_b, s_stats, s_store, s_ln,
                                   s_y_free).then_inc(s_fin, 1)

            run(dve, prologue, step, epilogue)


def ffn_phase(nc, tag, B, src, w1, b1, w2, b2, ln, dst, ahead, use):
    F = w1.shape[0]
    FC = F // P
    HJ = FC // 2
    W1N, W2N = KC * F, FC * D
    assert B >= 3

    with ExitStack() as ctx:
        def sb(name, shape, dt):
            return ctx.enter_context(nc.sbuf_tensor(tag + name, shape, dt))

        def sem(name):
            return ctx.enter_context(nc.semaphore(tag + name))

        def pair(name, shape):
            return sb(name + "_hi", shape, F32R), sb(name + "_lo", shape, F32R)

        w1T = pair("w1T", [P, KC, F])
        w2T = pair("w2T", [P, FC, D])
        xT = pair("xT", [P, KC, S])
        hT = pair("hT", [P, FC, S])
        y, yo = ahead.buf[:, 0, :, :], ahead.buf[:, 1, :, :]
        hidden = ahead.buf[:, 2:4, :, :].rearrange("p n t (c s) -> p (n t) c s", c=2)
        X_SLOT = Ahead.SLOTS - 1
        x_raw = ahead.buf[:, X_SLOT, :, :]
        ident = sb("ident", [P, P], F32)
        b1c = sb("b1c", [P, FC], F32)
        b2b = sb("b2b", [P, D], F32)
        ln_g = sb("ln_g", [P, D], F32)
        ln_b = sb("ln_b", [P, D], F32)
        stats = sb("stats", [P, TB, 6], F32)
        mv = sb("mv", [P, TB, 2], F32)
        ve = sb("ve", [P, TB], F32)
        rs = sb("rs", [P, TB], F32)
        ntmp = sb("ntmp", [P, TB], F32)
        NB = 4
        job_ps = [ctx.enter_context(nc.psum_tensor(f"{tag}job{n}", [P, 512], F32)) for n in range(NB)]

        s_ident = sem("s_ident")
        s_small = sem("s_small")
        s_w = [sem(f"s_w{n}") for n in range(FC // 2)]
        s_x = sem("s_x")
        s_job = sem("s_job")
        s_job_hi = sem("s_job_hi")
        s_job_done = sem("s_job_done")
        s_split = sem("s_split")
        s_yinit = sem("s_yinit")
        s_bn = sem("s_bn")
        s_stats = sem("s_stats")
        s_ln = sem("s_ln")
        s_y_free = sem("s_y_free")
        s_fin = sem("s_fin")
        s_store = sem("s_store")

        W_JOBS = [("w1T", r) for r in range(FC)] + [("w2T", (r, g)) for r in range(D // P) for g in range(KC)]
        PRO = W_JOBS + [("xT", 0), ("xT", 1)]

        def entry_jobs(last):
            return [("h", n) for n in range(HJ)] + ([] if last else [("xT", 0), ("xT", 1)]) + [("y", 0), ("y", 1)]

        N = len(entry_jobs(False))
        assert N % NB == 0

        N_HI = sum(kind != "y" for kind, _ in entry_jobs(False))
        PRO_HI = len(PRO)

        def run(eng, job, after):
            n = 0
            for kind, arg in PRO:
                job(kind, arg, n, n + 1, None, n % NB, PRO[n - 1][0] if n else None)
                n += 1

            def entry(b, last):
                prev = "xT" if isinstance(b, int) and b == 0 else "y"
                hi = 0
                for i, (kind, arg) in enumerate(entry_jobs(last)):
                    hi += kind != "y"
                    job(kind, arg, len(PRO) + b * N + i, PRO_HI + b * N_HI + hi, b,
                        (len(PRO) + i) % NB, prev)
                    prev = kind
                after(b, len(PRO) + b * N + len(entry_jobs(last)))

            entry(0, False)
            with eng.Fori(1, B - 1) as b:
                entry(b, False)
            entry(B - 1, True)

        block = ctx.enter_context(nc.Block())

        @block.sync
        def _(sp):
            x_v = src.rearrange("b (t p) f -> b p t f", p=P)
            dst_v = dst.rearrange("b (t p) f -> b p t f", p=P)
            for i in range(len(W_JOBS) // 2 - Ahead.SLOTS):
                sp.wait_ge(s_job, 2 * (i % X_SLOT + 1 + (Ahead.SLOTS if i >= X_SLOT else 0)))
                r, half = i // 2, i % 2
                piece = w2[r * P:(r + 1) * P, half * 2 * D:(half + 1) * 2 * D].rearrange("p (t f) -> p t f", t=2)
                sp.dma_start(ahead.buf[:, i % X_SLOT, :, :], piece).then_inc(s_w[i], 16)

            def load(b):
                sp.dma_start(x_raw[:, :, :], x_v[b]).then_inc(s_x, 16)

            def store(b):
                sp.wait_ge(s_fin, b + 1)
                sp.dma_start(dst_v[b], yo[:, :, :]).then_inc(s_store, 16)

            sp.wait_ge(s_job, 2 * Ahead.SLOTS)
            load(0)
            with nc.allow_non_contiguous_dma("a column per chunk"):
                sp.dma_start(b1c[:, :], b1.rearrange("(c p) -> p c", p=P)).then_inc(s_small, 16)
            sp.dma_start(b2b[:, :], b2.partition_broadcast(P)).then_inc(s_small, 16)
            sp.dma_start(ln_g[:, :], ln[0].partition_broadcast(P)).then_inc(s_small, 16)
            sp.dma_start(ln_b[:, :], ln[1].partition_broadcast(P)).then_inc(s_small, 16)
            sp.wait_ge(s_yinit, 1)
            load(1)
            with sp.Fori(1, B - 1) as b:
                sp.wait_ge(s_yinit, b + 1)
                load(b + 1)
                store(b - 1)
            store(B - 2)
            store(B - 1)
            sp.wait_ge(s_store, 16 * B)

        @block.gpsimd
        def _(pool):
            make_identity(pool, ident, s_ident)

            def finish(b):
                pool.wait_ge(s_stats, b + 1)
                if not (isinstance(b, int) and b == 0):
                    pool.wait_ge(s_store, 16 * b)
                pool.nop(nofuse=True)
                layernorm_apply(pool, y, yo, mv, ve, rs, ntmp, ln_g, ln_b,
                                chain_on(pool, s_ln, b * LN_CHAIN), s_y_free).then_inc(s_fin, 1)

            pool.wait_ge(s_small, 16 * 4)
            finish(0)
            with pool.Fori(1, B - 1) as b:
                finish(b)

        @block.tensor
        def _(pe):
            def job(kind, arg, n, _, b, slot, prev):
                bank = job_ps[slot]
                last_h = n - (0 if prev == "h" else 2)
                if (kind, prev) == ("h", "xT"):
                    pe.wait_ge(s_job_done, n)
                elif (kind, arg) == ("y", 0):
                    pe.wait_ge(s_job_done, last_h - 1)
                elif (kind, arg) == ("h", 0):
                    pe.wait_ge(s_job_done, n - 2)
                elif b is not None or n >= NB:
                    pe.wait_ge(s_job_done, n - NB + 1)
                if kind == "w1T":
                    if n % 2 == 0:
                        pe.wait_ge(ahead.loaded[n // 2], 16 * use)
                    tiles = [ahead.buf[:, n // 2, n % 2, c * P:(c + 1) * P] for c in range(KC)]
                elif kind == "w2T":
                    i = n // 2 - Ahead.SLOTS
                    if n % 2 == 0:
                        pe.wait_ge(s_w[i], 16)
                    tiles = [ahead.buf[:, i % X_SLOT, n % 2, c * P:(c + 1) * P] for c in range(KC)]
                elif kind == "xT":
                    nb = 0 if b is None else b + 1
                    pe.wait_ge(s_x, (nb + 1) * 16)
                    tiles = [x_raw[:, t, c * P:(c + 1) * P] for c in (2 * arg, 2 * arg + 1) for t in range(TB)]
                if kind in ("w1T", "w2T", "xT"):
                    for m, tile in enumerate(tiles):
                        mm = pe.transpose(bank[:, m * P:(m + 1) * P], tile, ident[:, :])
                elif kind == "h":
                    for c in range(2):
                        f = (2 * arg + c) * P
                        for kc in range(KC):
                            mm = matmul3(pe, bank[:, c * S:(c + 1) * S], [x[:, kc, f:f + P] for x in w1T],
                                         [x[:, kc, :] for x in xT], kc == 0, kc == KC - 1)
                else:
                    for fc in range(FC):
                        if arg == 0 and fc == FC - 2:
                            pe.wait_ge(s_job_done, last_h)
                        mm = matmul3(pe, bank[:, :], [x[:, fc, arg * P:(arg + 1) * P] for x in hT],
                                     [x[:, fc, :] for x in w2T], fc == 0, fc == FC - 1)
                mm.then_inc(s_job, 1)

            pe.wait_ge(s_ident, 2)
            run(pe, job, lambda b, n: None)

        def transposed(part, kind, arg):
            if kind == "w1T":
                return w1T[part][:, :, arg * P:(arg + 1) * P]
            if kind == "w2T":
                r, g = arg
                return w2T[part][:, g * KC:(g + 1) * KC, r * P:(r + 1) * P]
            return xT[part][:, 2 * arg:2 * arg + 2, :]

        def bank_view(bank, kind):
            return bank[:, :].rearrange("p (c f) -> p c f", c=2 if kind == "xT" else KC)

        @block.scalar
        def _(act):
            def job(kind, arg, n, _, b, slot, prev):
                if kind == "y":
                    return
                bank = job_ps[slot]
                act.wait_ge(s_job, n + 1)
                if kind == "h":
                    if isinstance(b, int) and (b, arg) == (0, 0):
                        act.wait_ge(s_small, 16 * 4)
                    for c in range(2):
                        m = 2 * arg + c
                        hi = act.activation(hidden[:, slot, c, :], bank[:, c * S:(c + 1) * S], ACT.Relu,
                                            bias=b1c[:, m:m + 1])
                else:
                    hi = act.activation(transposed(0, kind, arg), bank_view(bank, kind), ACT.Copy)
                hi.then_inc(s_job_hi, 1)

            run(act, job, lambda b, n: None)

        @block.vector
        def _(dve):
            def job(kind, arg, n, hi_jobs, b, slot, prev):
                bank = job_ps[slot]
                if kind == "y":
                    dve.wait_ge(s_job, n + 1)
                    lo = dve.tensor_tensor(y[:, arg, :], y[:, arg, :], bank[:, :], ALU.add)
                else:
                    if (kind, arg) == ("h", HJ // 2 - 1):
                        residual(b)
                    dve.wait_ge(s_job_hi, hi_jobs)
                    if kind == "h":
                        sl = slice(2 * arg, 2 * arg + 2)
                        dve.tensor_copy(hT[0][:, sl, :], hidden[:, slot, :, :]).then_inc(s_split, 1)
                        dve.wait_ge(s_split, b * HJ + arg + 1)
                        lo = dve.tensor_tensor(hT[1][:, sl, :], hidden[:, slot, :, :], hT[0][:, sl, :],
                                               ALU.subtract)
                    else:
                        lo = dve.tensor_tensor(transposed(1, kind, arg), bank_view(bank, kind),
                                               transposed(0, kind, arg), ALU.subtract)
                lo.then_inc(s_job_done, 1)

            def residual(b):
                if not (isinstance(b, int) and b == 0):
                    dve.wait_ge(s_y_free, b)
                else:
                    dve.wait_ge(s_small, 16 * 4)
                dve.tensor_tensor(y[:, :, :], x_raw[:, :, :], b2b[:, :].unsqueeze(1).to_broadcast([P, TB, D]),
                                  ALU.add).then_inc(s_yinit, 1)
                dve.wait_ge(s_yinit, b + 1)

            def statistics(b, jobs):
                dve.wait_ge(s_job_done, jobs)
                if not (isinstance(b, int) and b == 0):
                    dve.wait_ge(s_ln, b * LN_CHAIN)
                for t in range(TB):
                    row_stats(dve, y, stats, s_bn, t)
                row_mean_variance(dve, stats, mv, s_bn, b, s_stats)

            run(dve, job, statistics)
            last_layernorm(dve, B, y, yo, mv, ve, rs, ntmp, ln_g, ln_b, s_stats, s_store, s_ln,
                           s_y_free).then_inc(s_fin, 1)


def xattn_decoder(nc, x, ctx_1024, mask_k, mask_qk, w, out):
    B = x.shape[0]

    def between(n):
        return nc.dram_tensor(f"x{n}", x.shape, F32, kind="Internal").ap()

    x1, x2, x3 = between(1), between(2), between(3)
    attention_phase(nc, "a0_", B, x, ctx_1024, [w[f"L0_xattn_w{n}"] for n in "qkvo"],
                    x1, 64, norm_w=w["L0_xattn_norm_w"])
    with ExitStack() as ctx:
        ahead = Ahead(nc, ctx)
        sa = [w[f"L1_xattn_sa_w{n}"] for n in "qkvo"]
        ca = [w[f"L1_xattn_ca_w{n}"] for n in "qkvo"]
        w1 = w["L1_xattn_ffn_w1"]
        assert w1.shape[0] == Ahead.SLOTS * TB * P
        attention_phase(nc, "a1_", B, x1, None, sa, x2, 32, bias=[w[f"L1_xattn_sa_b{n}"] for n in "qkvo"],
                        mask=mask_qk, ln=(w["L1_xattn_ln1_g"], w["L1_xattn_ln1_b"]),
                        ahead=ahead, use=1, next_pieces=row_pieces(ca))
        attention_phase(nc, "a2_", B, x2, ctx_1024, ca, x3, 32, bias=[w[f"L1_xattn_ca_b{n}"] for n in "qkvo"],
                        mask=mask_k, ln=(w["L1_xattn_ln2_g"], w["L1_xattn_ln2_b"]), ahead=ahead, use=2,
                        next_pieces=row_pieces([w1[n:n + D, :] for n in range(0, w1.shape[0], D)]))
        ffn_phase(nc, "f_", B, x3, w1, w["L1_xattn_ffn_b1"], w["L1_xattn_ffn_w2"], w["L1_xattn_ffn_b2"],
                  (w["L1_xattn_ln3_g"], w["L1_xattn_ln3_b"]), out, ahead, 3)


def kernel(**inputs):
    import numpy as np
    import concourse.bacc as bacc
    from concourse.bass_utils import run_bass_kernel_spmd

    nc = bacc.Bacc("TRN2", target_bir_lowering=False, num_devices=1)
    arrays, args = {}, {}
    for name, value in inputs.items():
        a = np.ascontiguousarray(value)
        arrays[f"in_{name}"] = a
        args[name] = nc.dram_tensor(f"in_{name}", a.shape, mybir.dt.from_np(a.dtype), kind="ExternalInput").ap()
    out = nc.dram_tensor("out", inputs["x"].shape, F32, kind="ExternalOutput").ap()
    xattn_decoder(nc, args["x"], args["ctx_1024"], args["mask_Bx1x1xS2_if1"], args["mask_Bx1xSxS2_if1"], args, out)
    return run_bass_kernel_spmd(nc, [arrays], core_ids=[0]).results[0]["out"]
```
